# Optimizing a Trainium2 kernel written in Bass

```python
import numpy as np
import jax
import jax.numpy as jnp

def _softmax(x, axis=-1):
    return jax.nn.softmax(x, axis=axis)

def _gelu(x):
    return jax.nn.gelu(x, approximate=True)

def _silu(x):
    return jax.nn.silu(x)

def _sigmoid(x):
    return jax.nn.sigmoid(x)

def _layernorm(x, axis=-1, eps=1e-05):
    m = jnp.mean(x, axis=axis, keepdims=True)
    v = jnp.var(x, axis=axis, keepdims=True)
    return (x - m) / jnp.sqrt(v + eps)

def _scatter_add(tgt, idx, src, axis=0):
    return tgt.at[idx].add(src)

def _segment_sum(src, seg, n):
    return jax.ops.segment_sum(src, seg, n)
kernel_name = 'mk_cond_seq_d1_seqx_r2_b88ca5'

def setup_inputs(seed: int=0):
    np.random.seed(seed)
    _w = jnp.asarray

    def _rec_inputs():
        import jax
        import jax.numpy as jnp
        _rk = jax.random.key(seed)
        x = -1.528e-05 + 0.9999 * jax.random.normal(jax.random.fold_in(_rk, 1), (64, 128, 1024), jnp.float32)
        _lenS = 128 - jax.random.randint(jax.random.fold_in(_rk, 7), (64,), 0, max(1, 128 // 4) + 1, jnp.int32)
        _lenS2 = 128 - jax.random.randint(jax.random.fold_in(_rk, 8), (64,), 0, max(1, 128 // 4) + 1, jnp.int32)
        itok_B_1_2 = jax.random.randint(jax.random.fold_in(_rk, 11), (64,), 1, 3, jnp.int32)
        return (x, itok_B_1_2)
    x, itok_B_1_2 = _rec_inputs()

    def _L0_cond_setup():
        import jax, jax.numpy as jnp
        import numpy as np
        H = 1024
        K = 512
        R = 3
        B = 8
        S = 1024
        LN_EPS = 1e-05
        key = jax.random.key(seed)
        ks = jax.random.split(key, 8)
        sd_d = 1.0 / np.sqrt(H)
        sd_u = 1.0 / np.sqrt(K)
        return {'role': jax.random.randint(ks[0], (B,), 0, R), 'hidden_states': jax.random.normal(ks[1], (B, S, H), dtype=jnp.float32), 'W_down': jax.random.uniform(ks[2], (R, H, K), jnp.float32, -sd_d, sd_d), 'b_down': jax.random.uniform(ks[3], (R, K), jnp.float32, -sd_d, sd_d), 'W_up': jax.random.uniform(ks[4], (R, K, H), jnp.float32, -sd_u, sd_u), 'b_up': jax.random.uniform(ks[5], (R, H), jnp.float32, -sd_u, sd_u), 'gamma': jnp.ones((R, H), jnp.float32), 'beta': jnp.zeros((R, H), jnp.float32)}
    _L0_cond_all = _L0_cond_setup()
    _L0_cond_in = {k: v for k, v in _L0_cond_all.items() if k in ('W_down', 'b_down', 'W_up', 'b_up', 'gamma', 'beta')}
    del _L0_cond_all
    return {'x': x, 'itok_B_1_2': itok_B_1_2, 'L0_cond_W_down': _L0_cond_in['W_down'], 'L0_cond_b_down': _L0_cond_in['b_down'], 'L0_cond_W_up': _L0_cond_in['W_up'], 'L0_cond_b_up': _L0_cond_in['b_up'], 'L0_cond_gamma': _L0_cond_in['gamma'], 'L0_cond_beta': _L0_cond_in['beta']}

def reference(x, itok_B_1_2, L0_cond_W_down, L0_cond_b_down, L0_cond_W_up, L0_cond_b_up, L0_cond_gamma, L0_cond_beta):
    import jax
    import jax.numpy as jnp

    def _L0_cond_ref(role, hidden_states, W_down, b_down, W_up, b_up, gamma, beta):
        import jax, jax.numpy as jnp
        import numpy as np
        H = 1024
        K = 512
        R = 3
        B = 8
        S = 1024
        LN_EPS = 1e-05
        h = jnp.einsum('bsh,bhk->bsk', hidden_states, W_down[role]) + b_down[role][:, None, :]
        h = jax.nn.gelu(h, approximate=False)
        u = jnp.einsum('bsk,bkh->bsh', h, W_up[role]) + b_up[role][:, None, :]
        y = hidden_states + u
        mean = jnp.mean(y, axis=-1, keepdims=True)
        var = jnp.mean(jnp.square(y - mean), axis=-1, keepdims=True)
        yn = (y - mean) * jax.lax.rsqrt(var + LN_EPS)
        return yn * gamma[role][:, None, :] + beta[role][:, None, :]
    x = _L0_cond_ref(itok_B_1_2, x, L0_cond_W_down, L0_cond_b_down, L0_cond_W_up, L0_cond_b_up, L0_cond_gamma, L0_cond_beta)
    return x

_drawn_inputs = setup_inputs


def setup_inputs(seed=0):
    import zlib

    import numpy as np

    out = dict(_drawn_inputs(seed))
    spreads = {'L0_cond_gamma': (1.0, 0.2), 'L0_cond_beta': (0.0, 0.1)}
    factors = {'L0_cond_b_down': 8.0}
    for name, (base, spread) in spreads.items():
        noise = np.random.default_rng([zlib.crc32(name.encode()), seed]).standard_normal(out[name].shape)
        drawn = base * np.exp(spread * noise) if base else spread * noise
        out[name] = jnp.asarray(drawn.astype(out[name].dtype))
    for name, factor in factors.items():
        out[name] = (out[name] * factor).astype(out[name].dtype)
    return out
```

```python
from contextlib import ExitStack

import concourse.bass as bass
from concourse import mybir
from concourse.alu_op_type import AluOpType as ALU

F32 = mybir.dt.float32
F16 = mybir.dt.float16
I32 = mybir.dt.int32
ACT = mybir.ActivationFunctionType
AX_X = mybir.AxisListType.X
ABSMAX = bass.bass_isa.ReduceOp.absmax

P = 128
HI, LO = 0, 1
DOWN, UP = 0, 1
LN_EPS = 1e-5
EXPONENT_BITS = 0x7F800000
TINIEST = 2.0 ** -100
TOP = 2.0 ** 14
DMA = 16
RING = 4


def adapter(nc, x, role, w_down, b_down, w_up, b_up, gamma, beta, out):
    N, S, H = x.shape
    R, _, K = w_down.shape
    HC, KC = H // P, K // P
    WSIZE = H * K // P
    HALF = 512
    assert S == P and K == HALF and H == 2 * HALF and N % RING == 0

    PREP = [(r, m) for r in reversed(range(R)) for m in (DOWN, UP)]
    STAGED_IN = [None, (0, UP), (0, DOWN), None, (0, UP), None]
    STAGED_AFTER = {3: 1, 4: 2, 5: 4}

    with ExitStack() as ctx:
        def sb(name, shape, dt):
            return ctx.enter_context(nc.sbuf_tensor(name, shape, dt))

        def psum(name, shape, dt):
            return ctx.enter_context(nc.psum_tensor(name, shape, dt))

        def sem(name):
            return ctx.enter_context(nc.semaphore(name))

        weights = sb("weights", [P, R * 2 * 2 * WSIZE], F16)
        stage = sb("stage", [P, WSIZE], F32)
        bdown_all = sb("bdown_all", [P, R * K], F32)
        bup_all = sb("bup_all", [P, R * H], F32)
        gamma_all = sb("gamma_all", [P, R * H], F32)
        beta_all = sb("beta_all", [P, R * H], F32)
        xs = sb("xs", [P, RING, H], F32)
        x16 = sb("x16", [P, 2, H], F16)
        xT = sb("xT", [P, 2, 2, HC, P], F16)
        hs = sb("hs", [P, 2, K], F32)
        h16 = sb("h16", [P, 2, 2, K], F16)
        hT = sb("hT", [P, 2, 2, KC, P], F16)
        ys = sb("ys", [P, 2, H], F32)
        ident = sb("ident", [P, P], F16)
        roles = sb("roles", [1, N], I32)
        role_tmp = sb("role_tmp", [1, 2, N], I32)
        wmax = sb("wmax", [P, 2 * R], F32)
        wpow = sb("wpow", [P, 2, 2 * R], F32)
        w_scale = sb("w_scale", [P, 2 * R], F32)
        w_inv = sb("w_inv", [P, 2 * R], F32)
        xst = sb("xst", [P, RING, 4], F32)
        hst = sb("hst", [P, RING, 4], F32)
        undo = sb("undo", [P, RING, 2], F32)
        stats = sb("stats", [P, RING, 2, 6], F32)
        moments = sb("moments", [P, RING, 2], F32)
        norm = sb("norm", [P, RING, 4], F32)
        minus_half = sb("minus_half", [P, 1], F32)
        eps = sb("eps", [P, 1], F32)

        z_ps = psum("z_ps", [P, K], F32)
        u_ps = psum("u_ps", [P, H], F32)
        xT_ps = psum("xT_ps", [P, 2, HC, P], F16)
        hT_ps = psum("hT_ps", [P, 2, KC, P], F16)

        roles_loaded, tables_loaded = sem("roles_loaded"), sem("tables_loaded")
        role_step, roles_ready = sem("role_step"), sem("roles_ready")
        ident_zero, ident_ready, half_ready = sem("ident_zero"), sem("ident_ready"), sem("half_ready")
        w_loaded = [sem(f"w_loaded{m}") for m in range(2 * R)]
        wmax_ready, wall_ready, wpow_ready = sem("wmax_ready"), sem("wall_ready"), sem("wpow_ready")
        winv_ready, wscale_ready = sem("winv_ready"), sem("wscale_ready")
        whi_ready, wlo_ready = sem("whi_ready"), sem("wlo_ready")
        x_loaded = [sem(f"x_loaded{j}") for j in range(RING)]
        xmax_ready, xpow_ready, xinv_ready = sem("xmax_ready"), sem("xpow_ready"), sem("xinv_ready")
        xscale_ready, xhi_ready, xlo_ready = sem("xscale_ready"), sem("xhi_ready"), sem("xlo_ready")
        xres_ready = sem("xres_ready")
        xT_hi_done, xT_lo_done = sem("xT_hi_done"), sem("xT_lo_done")
        xT_hi_ready, xT_lo_ready = sem("xT_hi_ready"), sem("xT_lo_ready")
        z_done, zundo_ready, z_ready, h_ready = sem("z_done"), sem("zundo_ready"), sem("z_ready"), sem("h_ready")
        hmax_ready, hpow_ready, hinv_ready = sem("hmax_ready"), sem("hpow_ready"), sem("hinv_ready")
        hscale_ready, hhi_ready, hlo_ready = sem("hscale_ready"), sem("hhi_ready"), sem("hlo_ready")
        hT_done, hT_ready = sem("hT_done"), sem("hT_ready")
        u_done, uundo_ready, y_ready = sem("u_done"), sem("uundo_ready"), sem("y_ready")
        stats_ready, moments_ready = sem("stats_ready"), sem("moments_ready")
        veps_ready, neg_ready, rstd_ready, norm_ready = sem("veps_ready"), sem("neg_ready"), sem("rstd_ready"), sem("norm_ready")
        yn_ready, scaled_ready, result_ready = sem("yn_ready"), sem("scaled_ready"), sem("result_ready")
        stored = [sem(f"stored{j}") for j in range(2)]

        def w_at(r, m, part, first, count):
            return weights[:, bass.ds(r * (4 * WSIZE) + ((2 * m + part) * WSIZE + first), count)]

        def staging(i):
            if STAGED_IN[i] is None:
                return stage[:, :]
            r, m = STAGED_IN[i]
            at = (2 * r + m) * 2 * WSIZE
            return weights[:, at:at + 2 * WSIZE].bitcast(F32)

        def run(eng, step, last):
            for s in range(RING):
                step(s, s)
            with eng.Fori(1, N // RING - 1) as k:
                for j in range(RING):
                    step(k * RING + j, j)
            for s in range(N - RING, last):
                step(s, s % RING)

        block = ctx.enter_context(nc.Block())

        @block.sync
        def _(sp):
            sp.dma_start(roles[:, :], role.rearrange("(o n) -> o n", o=1)).then_inc(roles_loaded, DMA)

            def load_w(i):
                r, m = PREP[i]
                src = (w_down if m == DOWN else w_up)[r].rearrange("(c p) k -> p c k", p=P)
                dst = staging(i).rearrange("p (c k) -> p c k", c=HC if m == DOWN else KC)
                sp.dma_start(dst, src).then_inc(w_loaded[i], DMA)

            def load_x(s, j):
                sp.dma_start(xs[:, j, :], x[s]).then_inc(x_loaded[j], DMA)

            load_w(0)
            load_w(1)
            load_w(2)
            for j in range(RING):
                load_x(j, j)
            for dst, src in ((bdown_all, b_down), (bup_all, b_up), (gamma_all, gamma), (beta_all, beta)):
                sp.dma_start(dst[:, :], src.rearrange("(o r) n -> o (r n)", o=1).partition_broadcast(P)
                             ).then_inc(tables_loaded, DMA)
            for i in range(3, 2 * R):
                sp.wait_ge(whi_ready, STAGED_AFTER[i])
                sp.wait_ge(wlo_ready, STAGED_AFTER[i])
                load_w(i)

            def step(s, j):
                if not isinstance(s, int) or s + RING < N:
                    sp.wait_ge(y_ready, s + 1)
                    sp.dma_start(xs[:, j, :], x[bass.ds(s + RING, 1)].rearrange("o p h -> (o p) h")
                                 ).then_inc(x_loaded[j], DMA)
                sp.wait_ge(result_ready, s + 1)
                sp.dma_start(out[bass.ds(s, 1)].rearrange("o p h -> (o p) h"), ys[:, j % 2, :]
                             ).then_inc(stored[j % 2], DMA)

            run(sp, step, N)
            for j in range(2):
                sp.wait_ge(stored[j], DMA * (N // 2))

        @block.gpsimd
        def _(pool):
            pool.memset(minus_half[:, :], -0.5).then_inc(half_ready, 1)
            pool.memset(eps[:, :], LN_EPS).then_inc(half_ready, 1)
            pool.memset(ident[:, :], 0.0).then_inc(ident_zero, 1)
            pool.wait_ge(ident_zero, 1)
            pool.affine_select(out=ident[:, :], in_=ident[:, :], compare_op=ALU.not_equal, fill=1.0, base=0,
                               pattern=[[-1, P]], channel_multiplier=1).then_inc(ident_ready, 1)
            for i in range(2 * R):
                pool.wait_ge(wmax_ready, i + 1)
                pool.partition_all_reduce(wpow[:, 0, i:i + 1], wmax[:, i:i + 1], P, ABSMAX).then_inc(wall_ready, 1)
            pool.wait_ge(roles_ready, 1)
            pool.wait_ge(half_ready, 2)

            def step(i, j):
                if not isinstance(i, int) or i < N:
                    r = pool.value_load(roles[0:1, bass.ds(i, 1)], min_val=0, max_val=R - 1)
                    pool.wait_ge(xhi_ready, i + 1)
                    pool.wait_ge(xlo_ready, i + 1)
                    pool.wait_ge(tables_loaded, 4 * DMA)
                    pool.tensor_tensor(xs[:, j, :], xs[:, j, :], bup_all[:, bass.ds(r * H, H)], ALU.add
                                       ).then_inc(xres_ready, 1)
                if not isinstance(i, int) or i >= 2:
                    s, js = i - 2, (j - 2) % RING
                    r = pool.value_load(roles[0:1, bass.ds(s, 1)], min_val=0, max_val=R - 1)
                    pool.wait_ge(moments_ready, s + 1)
                    pool.tensor_tensor(norm[:, js, 0:1], moments[:, js, 1:2], eps[:, :], ALU.add
                                       ).then_inc(veps_ready, 1)
                    pool.tensor_scalar(norm[:, js, 2:3], moments[:, js, 0:1], -1.0, None, ALU.mult
                                       ).then_inc(neg_ready, 1)
                    pool.wait_ge(veps_ready, s + 1)
                    pool.tensor_tensor(norm[:, js, 1:2], norm[:, js, 0:1], minus_half[:, :], ALU.pow
                                       ).then_inc(rstd_ready, 1)
                    pool.wait_ge(rstd_ready, s + 1)
                    pool.wait_ge(neg_ready, s + 1)
                    pool.tensor_tensor(norm[:, js, 3:4], norm[:, js, 2:3], norm[:, js, 1:2], ALU.mult
                                       ).then_inc(norm_ready, 1)
                    pool.wait_ge(yn_ready, s + 1)
                    pool.wait_ge(tables_loaded, 4 * DMA)
                    pool.tensor_tensor(ys[:, js % 2, :], ys[:, js % 2, :], gamma_all[:, bass.ds(r * H, H)],
                                       ALU.mult).then_inc(scaled_ready, 1)
                    pool.wait_ge(scaled_ready, s + 1)
                    pool.wait_ge(tables_loaded, 4 * DMA)
                    pool.tensor_tensor(ys[:, js % 2, :], ys[:, js % 2, :], beta_all[:, bass.ds(r * H, H)],
                                       ALU.add).then_inc(result_ready, 1)

            run(pool, step, N + 2)

        @block.scalar
        def _(act):
            for i, (r, m) in enumerate(PREP):
                act.wait_ge(wscale_ready, i + 1)
                act.activation(w_at(r, m, HI, 0, WSIZE), staging(i), ACT.Copy, scale=w_scale[:, i:i + 1]
                               ).then_inc(whi_ready, 1)

            def split_x(s, j):
                act.wait_ge(xscale_ready, s + 1)
                if not isinstance(s, int) or s >= 1:
                    act.wait_ge(xT_hi_done, s)
                act.activation(x16[:, HI, :], xs[:, j, :], ACT.Copy, scale=xst[:, j, 3:4]).then_inc(xhi_ready, 1)

            def step(i, j):
                late = not isinstance(i, int)
                if late or i + 1 < N:
                    split_x(i + 1, (j + 1) % RING)
                if (late or i >= 1) and (late or i - 1 < N):
                    s, js = i - 1, (j - 1) % RING
                    act.wait_ge(hT_done, s + 1)
                    if late or s >= 2:
                        act.wait_ge(u_done, s - 1)
                    act.copy(hT[:, js % 2, :, :, :], hT_ps[:, :, :, :]).then_inc(hT_ready, 1)
                if late or i >= 2:
                    s, js = i - 2, (j - 2) % RING
                    act.wait_ge(norm_ready, s + 1)
                    act.activation(ys[:, js % 2, :], ys[:, js % 2, :], ACT.Identity, bias=norm[:, js, 3:4],
                                   scale=norm[:, js, 1:2]).then_inc(yn_ready, 1)
                if late or i + 1 < N:
                    copy_xT(i + 1, (j + 1) % RING)
                if late or i < N:
                    act.wait_ge(z_ready, i + 1)
                    act.activation(hs[:, j % 2, :], hs[:, j % 2, :], ACT.Gelu).then_inc(h_ready, 1)
                    act.wait_ge(hscale_ready, i + 1)
                    if late or i >= 2:
                        act.wait_ge(hT_done, i - 1)
                    act.activation(h16[:, j % 2, HI, :], hs[:, j % 2, :], ACT.Copy, scale=hst[:, j, 3:4]
                                   ).then_inc(hhi_ready, 1)

            def copy_xT(s, j):
                late = not isinstance(s, int)
                act.wait_ge(xT_hi_done, s + 1)
                if late or s >= 2:
                    act.wait_ge(z_done, s - 1)
                act.copy(xT[:, j % 2, HI, :, :], xT_ps[:, HI, :, :]).then_inc(xT_hi_ready, 1)
                act.wait_ge(xT_lo_done, s + 1)
                act.copy(xT[:, j % 2, LO, :, :], xT_ps[:, LO, :, :]).then_inc(xT_lo_ready, 1)

            split_x(0, 0)
            copy_xT(0, 0)
            run(act, step, N + 2)

        @block.vector
        def _(dve):
            dve.wait_ge(roles_loaded, DMA)
            dve.tensor_scalar(role_tmp[:, 0, :], roles[:, :], 0.0, float(R), ALU.is_lt, ALU.mult).then_inc(role_step, 1)
            dve.wait_ge(role_step, 1)
            dve.tensor_tensor(role_tmp[:, 1, :], roles[:, :], role_tmp[:, 0, :], ALU.add).then_inc(role_step, 1)
            dve.wait_ge(role_step, 2)
            dve.tensor_scalar(roles[:, :], role_tmp[:, 1, :], 0.0, float(R - 1), ALU.max, ALU.min).then_inc(roles_ready, 1)

            def power_scales(count, top, power, inverse, scale, pow_ready, inv_ready, scale_ready):
                dve.tensor_scalar(power.bitcast(I32), top.bitcast(I32), EXPONENT_BITS, None, ALU.bitwise_and
                                  ).then_inc(pow_ready, 1)
                dve.wait_ge(pow_ready, count)
                dve.tensor_scalar(inverse, power, TINIEST, 1.0 / TOP, ALU.max, ALU.mult).then_inc(inv_ready, 1)
                dve.wait_ge(inv_ready, count)
                dve.reciprocal(scale, inverse).then_inc(scale_ready, 1)

            def largest_w(i):
                dve.wait_ge(w_loaded[i], DMA)
                dve.tensor_reduce(wmax[:, i:i + 1], staging(i), AX_X, ALU.max, apply_absolute_value=True
                                  ).then_inc(wmax_ready, 1)

            def split_w(i):
                dve.wait_ge(wall_ready, i + 1)
                r, m = PREP[i]
                c = 2 * r + m
                power_scales(i + 1, wpow[:, 0, i:i + 1], wpow[:, 1, i:i + 1], w_inv[:, c:c + 1],
                             w_scale[:, i:i + 1], wpow_ready, winv_ready, wscale_ready)
                dve.wait_ge(whi_ready, i + 1)
                dve.scalar_tensor_tensor(out=w_at(r, m, LO, 0, WSIZE), in0=staging(i), scalar=w_scale[:, i:i + 1],
                                         in1=w_at(r, m, HI, 0, WSIZE), op0=ALU.mult, op1=ALU.subtract
                                         ).then_inc(wlo_ready, 1)

            def make_moments(s, j):
                dve.bn_aggr(moments[:, j, :], stats[:, j, :, :]).then_inc(moments_ready, 1)

            def largest_x(s, j):
                late = not isinstance(s, int)
                dve.wait_ge(x_loaded[j], DMA * (s // RING + 1) if not late else (s - j) * (DMA // RING) + DMA)
                dve.tensor_reduce(xst[:, j, 0:1], xs[:, j, :], AX_X, ALU.max, apply_absolute_value=True
                                  ).then_inc(xmax_ready, 1)

            def split_x(s, j):
                late = not isinstance(s, int)
                dve.wait_ge(xmax_ready, s + 1)
                power_scales(s + 1, xst[:, j, 0:1], xst[:, j, 1:2], xst[:, j, 2:3], xst[:, j, 3:4],
                             xpow_ready, xinv_ready, xscale_ready)
                dve.wait_ge(xhi_ready, s + 1)
                if late or s >= 1:
                    dve.wait_ge(xT_lo_done, s)
                dve.scalar_tensor_tensor(out=x16[:, LO, :], in0=xs[:, j, :], scalar=xst[:, j, 3:4],
                                         in1=x16[:, HI, :], op0=ALU.mult, op1=ALU.subtract).then_inc(xlo_ready, 1)

            def make_z(s, j):
                r = dve.value_load(roles[0:1, bass.ds(s, 1)], min_val=0, max_val=R - 1)
                dve.tensor_tensor(undo[:, j, 0:1], xst[:, j, 2:3], w_inv[:, bass.ds(2 * r + DOWN, 1)], ALU.mult
                                  ).then_inc(zundo_ready, 1)
                dve.wait_ge(zundo_ready, s + 1)
                dve.wait_ge(z_done, s + 1)
                dve.scalar_tensor_tensor(out=hs[:, j % 2, :], in0=z_ps[:, :], scalar=undo[:, j, 0:1],
                                         in1=bdown_all[:, bass.ds(r * K, K)], op0=ALU.mult, op1=ALU.add
                                         ).then_inc(z_ready, 1)

            def split_h(s, j):
                dve.wait_ge(h_ready, s + 1)
                dve.tensor_reduce(hst[:, j, 0:1], hs[:, j % 2, :], AX_X, ALU.max, apply_absolute_value=True
                                  ).then_inc(hmax_ready, 1)
                dve.wait_ge(hmax_ready, s + 1)
                power_scales(s + 1, hst[:, j, 0:1], hst[:, j, 1:2], hst[:, j, 2:3], hst[:, j, 3:4],
                             hpow_ready, hinv_ready, hscale_ready)
                r = dve.value_load(roles[0:1, bass.ds(s, 1)], min_val=0, max_val=R - 1)
                dve.tensor_tensor(undo[:, j, 1:2], hst[:, j, 2:3], w_inv[:, bass.ds(2 * r + UP, 1)], ALU.mult
                                  ).then_inc(uundo_ready, 1)
                dve.wait_ge(hhi_ready, s + 1)
                dve.scalar_tensor_tensor(out=h16[:, j % 2, LO, :], in0=hs[:, j % 2, :], scalar=hst[:, j, 3:4],
                                         in1=h16[:, j % 2, HI, :], op0=ALU.mult, op1=ALU.subtract
                                         ).then_inc(hlo_ready, 1)

            def make_y(s, j):
                late = not isinstance(s, int)
                dve.wait_ge(u_done, s + 1)
                dve.wait_ge(uundo_ready, s + 1)
                dve.wait_ge(xres_ready, s + 1)
                if late or s >= 2:
                    dve.wait_ge(stored[j % 2], DMA * (s // 2) if not late else (s - j % 2) * (DMA // 2))
                dve.scalar_tensor_tensor(out=ys[:, j % 2, :], in0=u_ps[:, :], scalar=undo[:, j, 1:2],
                                         in1=xs[:, j, :], op0=ALU.mult, op1=ALU.add).then_inc(y_ready, 1)
                dve.wait_ge(y_ready, s + 1)
                for c in range(2):
                    dve.bn_stats(stats[:, j, c, :], ys[:, j % 2, c * HALF:(c + 1) * HALF]).then_inc(stats_ready, 1)

            def step(i, j):
                late = not isinstance(i, int)
                if late or i >= 2:
                    make_y(i - 2, (j - 2) % RING)
                    dve.wait_ge(stats_ready, 2 * (i - 2) + 2)
                if late or i + 1 < N:
                    largest_x(i + 1, (j + 1) % RING)
                if late or i >= 2:
                    make_moments(i - 2, (j - 2) % RING)
                if late or i + 1 < N:
                    split_x(i + 1, (j + 1) % RING)
                if late or i < N:
                    make_z(i, j)
                    split_h(i, j)

            largest_w(0)
            largest_w(1)
            for i in range(2 * R):
                split_w(i)
                if i + 2 < 2 * R:
                    largest_w(i + 2)
            dve.wait_ge(tables_loaded, 4 * DMA)
            largest_x(0, 0)
            split_x(0, 0)
            run(dve, step, N + 2)

        @block.tensor
        def _(pe):
            pe.wait_ge(ident_ready, 1)
            pe.wait_ge(roles_ready, 1)

            def transpose_x(s, j):
                late = not isinstance(s, int)
                pe.wait_ge(xhi_ready, s + 1)
                if late or s >= 1:
                    pe.wait_ge(xT_hi_ready, s)
                for c in range(HC):
                    t = pe.transpose(xT_ps[:, HI, c, :], x16[:, HI, c * P:(c + 1) * P], ident[:, :])
                t.then_inc(xT_hi_done, 1)
                pe.wait_ge(xlo_ready, s + 1)
                if late or s >= 1:
                    pe.wait_ge(xT_lo_ready, s)
                for c in range(HC):
                    t = pe.transpose(xT_ps[:, LO, c, :], x16[:, LO, c * P:(c + 1) * P], ident[:, :])
                t.then_inc(xT_lo_done, 1)

            def transpose_h(s, j):
                late = not isinstance(s, int)
                pe.wait_ge(hhi_ready, s + 1)
                pe.wait_ge(hlo_ready, s + 1)
                if late or s >= 1:
                    pe.wait_ge(hT_ready, s)
                for part in (HI, LO):
                    for c in range(KC):
                        t = pe.transpose(hT_ps[:, part, c, :], h16[:, j % 2, part, c * P:(c + 1) * P], ident[:, :])
                t.then_inc(hT_done, 1)

            def down(s, j, r, chunks):
                for c in chunks:
                    for a, w in ((HI, HI), (HI, LO), (LO, HI)):
                        t = pe.matmul(z_ps[:, :], xT[:, j % 2, a, c, :], w_at(r, DOWN, w, c * K, K),
                                      start=(c == 0 and a == HI and w == HI), stop=(c == HC - 1 and a == LO))
                if chunks[-1] == HC - 1:
                    t.then_inc(z_done, 1)

            def up(s, j):
                late = not isinstance(s, int)
                r = pe.value_load(roles[0:1, bass.ds(s, 1)], min_val=0, max_val=R - 1)
                pe.wait_ge(hT_ready, s + 1)
                if late or s >= 1:
                    pe.wait_ge(y_ready, s)
                for c in range(KC):
                    for a, w in ((HI, HI), (HI, LO), (LO, HI)):
                        for n in range(H // HALF):
                            t = pe.matmul(u_ps[:, n * HALF:(n + 1) * HALF], hT[:, j % 2, a, c, :],
                                          w_at(r, UP, w, c * H + n * HALF, HALF),
                                          start=(c == 0 and a == HI and w == HI), stop=(c == KC - 1 and a == LO))
                t.then_inc(u_done, 1)

            def step(i, j):
                late = not isinstance(i, int)
                if late or i < N:
                    r = pe.value_load(roles[0:1, bass.ds(i, 1)], min_val=0, max_val=R - 1)
                    pe.wait_ge(xT_hi_ready, i + 1)
                    pe.wait_ge(xT_lo_ready, i + 1)
                    if late or i >= 1:
                        pe.wait_ge(z_ready, i)
                    down(i, j, r, range(0, HC // 2))
                if (late or i >= 1):
                    transpose_h(i - 1, (j - 1) % RING)
                if late or i < N:
                    down(i, j, r, range(HC // 2, HC))
                if late or i + 1 < N:
                    transpose_x(i + 1, (j + 1) % RING)
                if late or i >= 1:
                    up(i - 1, (j - 1) % RING)

            transpose_x(0, 0)
            pe.wait_ge(whi_ready, 2 * R)
            pe.wait_ge(wlo_ready, 2 * R)
            run(pe, step, N + 1)


_INS = ["x", "itok_B_1_2", "L0_cond_W_down", "L0_cond_b_down", "L0_cond_W_up", "L0_cond_b_up",
        "L0_cond_gamma", "L0_cond_beta"]
_OUT = ((64, 128, 1024), "float32")


def kernel(**inputs):
    import numpy as _np
    import concourse.bacc as _bacc
    from concourse import mybir as _mybir
    from concourse.bass_utils import run_bass_kernel_spmd as _run

    nc = _bacc.Bacc("TRN2", target_bir_lowering=False, num_devices=1)
    arrays, args = {}, []
    for name in _INS:
        a = _np.ascontiguousarray(inputs[name])
        arrays[f"in_{name}_dram"] = a
        args.append(nc.dram_tensor(f"in_{name}_dram", a.shape, _mybir.dt.from_np(a.dtype), kind="ExternalInput").ap())
    shape, dtype = _OUT
    args.append(nc.dram_tensor("out_0_dram", shape, _mybir.dt.from_np(_np.dtype(dtype)), kind="ExternalOutput").ap())
    adapter(nc, *args)
    r = _run(nc, [arrays], core_ids=[0])
    return r.results[0]["out_0_dram"]
```

```python
from contextlib import ExitStack

import concourse.bass as bass
from concourse import mybir
from concourse.alu_op_type import AluOpType as ALU

F32 = mybir.dt.float32
F16 = mybir.dt.float16
I32 = mybir.dt.int32
ACT = mybir.ActivationFunctionType
AX_X = mybir.AxisListType.X
ABSMAX = bass.bass_isa.ReduceOp.absmax

P = 128
HI, LO = 0, 1
DOWN, UP = 0, 1
LN_EPS = 1e-5
EXPONENT_BITS = 0x7F800000
TINIEST = 2.0 ** -100
TOP = 2.0 ** 14
DMA = 16
UNROLL = 6
PEELED = 4


class Slot:

    def __init__(self, k, c, stride=UNROLL):
        self.k, self.c, self.stride, self.loop = k, c, stride, not isinstance(k, int)
        self.at = k * stride + c

    def __add__(self, d):
        return Slot(self.k, self.c + d, self.stride)

    def __sub__(self, d):
        return Slot(self.k, self.c - d, self.stride)

    def since(self, first):
        return self.loop or self.c >= first

    def before(self, end):
        return self.loop or self.c < end

    def buf(self, ring):
        return self.c % ring

    def turn(self, ring):
        return self.k * (self.stride // ring) + self.c // ring


class Piece:

    def __init__(self, k, c):
        self.k, self.kind, self.phase = k, (c - PEELED) // UNROLL, (c - PEELED) % UNROLL
        self.matrix = k * 2 + self.kind


def adapter(nc, x, role, w_down, b_down, w_up, b_up, gamma, beta, out):
    N, S, H = x.shape
    R, _, K = w_down.shape
    HC, KC = H // P, K // P
    WSIZE = H * K // P
    QUARTER, HALF = WSIZE // 4, WSIZE // 2
    BANK = 512
    XRING, YRING = 6, 3
    STEPS_A = 2 * UNROLL
    LOOP_B = PEELED + (R - 1) * STEPS_A
    TRIPS_B = (N - XRING - LOOP_B) // UNROLL
    AFTER = LOOP_B + TRIPS_B * UNROLL
    assert S == P and K == BANK and H == 2 * BANK and R == 3 and N % 8 == 0
    assert PEELED + STEPS_A + UNROLL <= -(-N // R) and LOOP_B + UNROLL <= -(-2 * N // R)

    with ExitStack() as ctx:
        def sb(name, shape, dt):
            return ctx.enter_context(nc.sbuf_tensor(name, shape, dt))

        def psum(name, shape, dt):
            return ctx.enter_context(nc.psum_tensor(name, shape, dt))

        def sem(name):
            return ctx.enter_context(nc.semaphore(name))

        weights = sb("weights", [P, R * 2 * 2 * WSIZE], F16)
        stage = sb("stage", [P, WSIZE], F32)
        bdown_all = sb("bdown_all", [P, R * K], F32)
        bup_all = sb("bup_all", [P, R * H], F32)
        gamma_all = sb("gamma_all", [P, R * H], F32)
        beta_all = sb("beta_all", [P, R * H], F32)
        xs = sb("xs", [P, XRING, H], F32)
        x16 = sb("x16", [P, 2, 2, H], F16)
        xT = sb("xT", [P, 2, 2, HC, P], F16)
        hs = sb("hs", [P, 2, K], F32)
        h16 = sb("h16", [P, 2, 2, K], F16)
        hT = sb("hT", [P, 2, 2, KC, P], F16)
        ys = sb("ys", [P, YRING, H], F32)
        ident = sb("ident", [P, P], F16)

        carved = [0]

        def carve(*dims):
            at, size = carved[0], 1
            for d in dims:
                size *= d
            carved[0] = at + size
            assert carved[0] <= 2 * K
            flat = hs[0:1, :, :].rearrange("o a k -> o (a k)")[:, at:at + size]
            return flat.rearrange("o (a n) -> o a n", a=dims[0]) if len(dims) == 2 else flat

        role_in = sb("role_in", [1, N], I32)
        countdown = sb("countdown", [1, N + R], I32)
        role_f = carve(3, N)
        is_role = carve(R, N)
        per_role = carve(5, R)
        countdown_f = carve(N + R)
        picks = carve(R, R)
        picked = carve(R)
        rank_of = carve(R, N)
        keys = carve(2, N)
        order_f = carve(3, N)
        role_by_rank = sb("role_by_rank", [1, R], I32)
        rank_at = sb("rank_at", [1, N], I32)
        seq_at = sb("seq_at", [1, N], I32)

        first_max = sb("first_max", [P, 2, 4], F32)
        first_all = sb("first_all", [P, 2, 4], F32)
        wmax = sb("wmax", [P, 2], F32)
        wall = sb("wall", [P, 2], F32)
        wpow = sb("wpow", [P, 3], F32)
        w_scale = sb("w_scale", [P, 3], F32)
        w_inv = sb("w_inv", [P, 2 * R], F32)
        xst = sb("xst", [P, UNROLL, 4], F32)
        hst = sb("hst", [P, UNROLL, 4], F32)
        undo = sb("undo", [P, UNROLL, 2], F32)
        stats = sb("stats", [P, UNROLL, 2, 6], F32)
        moments = sb("moments", [P, UNROLL, 2], F32)
        norm = sb("norm", [P, UNROLL, 4], F32)
        minus_half = sb("minus_half", [P, 1], F32)
        eps = sb("eps", [P, 1], F32)

        z_ps = psum("z_ps", [P, 2, K], F32)
        u_ps = psum("u_ps", [P, H], F32)
        xT_ps = psum("xT_ps", [P, 2, HC, P], F16)
        hT_ps = psum("hT_ps", [P, 2, KC, P], F16)

        roles_loaded, chain, consts_ready = sem("roles_loaded"), sem("chain"), sem("consts_ready")
        countdown_ready, ranked, sorted_ready = sem("countdown_ready"), sem("ranked"), sem("sorted_ready")
        zeroed, ident_ready = sem("zeroed"), sem("ident_ready")
        bdown_loaded, tables_loaded, late_tables_loaded = (
            sem("bdown_loaded"), sem("tables_loaded"), sem("late_tables_loaded"))
        first_loaded = [[sem(f"first_loaded{m}{q}") for q in range(4)] for m in (DOWN, UP)]
        fmax_ready, fall_ready, ftop_ready = sem("fmax_ready"), sem("fall_ready"), sem("ftop_ready")
        fpow_ready, finv_ready, fscale_ready = sem("fpow_ready"), sem("finv_ready"), sem("fscale_ready")
        fhi_ready = sem("fhi_ready")
        w_loaded = [sem(f"w_loaded{h}") for h in range(2)]
        wmax_ready, wall_ready, wtop_ready = sem("wmax_ready"), sem("wall_ready"), sem("wtop_ready")
        wpow_ready, winv_ready, wscale_ready = sem("wpow_ready"), sem("winv_ready"), sem("wscale_ready")
        whi_ready, wtable_ready = sem("whi_ready"), sem("wtable_ready")
        wlo_ready = sem("wlo_ready")
        x_loaded = [sem(f"x_loaded{j}") for j in range(XRING)]
        xmax_ready, xpow_ready, xinv_ready = sem("xmax_ready"), sem("xpow_ready"), sem("xinv_ready")
        xscale_ready, xhi_ready, xlo_ready = sem("xscale_ready"), sem("xhi_ready"), sem("xlo_ready")
        xres_ready = sem("xres_ready")
        xT_hi_done, xT_lo_done = sem("xT_hi_done"), sem("xT_lo_done")
        xT_hi_ready, xT_lo_ready = sem("xT_hi_ready"), sem("xT_lo_ready")
        z_done, zundo_ready, z_ready, h_ready = sem("z_done"), sem("zundo_ready"), sem("z_ready"), sem("h_ready")
        hmax_ready, hpow_ready, hinv_ready = sem("hmax_ready"), sem("hpow_ready"), sem("hinv_ready")
        hscale_ready, hhi_ready, hlo_ready = sem("hscale_ready"), sem("hhi_ready"), sem("hlo_ready")
        hT_done, hT_ready = sem("hT_done"), sem("hT_ready")
        u_done, uundo_ready, y_ready = sem("u_done"), sem("uundo_ready"), sem("y_ready")
        stats_ready, moments_ready = sem("stats_ready"), sem("moments_ready")
        veps_ready, neg_ready, rstd_ready = sem("veps_ready"), sem("neg_ready"), sem("rstd_ready")
        norm_ready = sem("norm_ready")
        yn_ready, scaled_ready, result_ready = sem("yn_ready"), sem("scaled_ready"), sem("result_ready")
        stored = [sem(f"stored{j}") for j in range(YRING)]

        def w_at(rank, m, part, first, count):
            return weights[:, bass.ds(rank * (4 * WSIZE) + ((2 * m + part) * WSIZE + first), count)]

        def first_staging(m, first, count):
            if m == DOWN:
                return stage[:, first:first + count]
            at = ((R - 1) * 2 + UP) * 2 * WSIZE
            return weights[:, at:at + 2 * WSIZE].bitcast(F32)[:, first:first + count]

        def source(r, m, first, count):
            w, width = ((w_down, K), (w_up, H))[m]
            rows = w[bass.ds(r, 1), first // width * P:(first + count) // width * P, :]
            return rows.rearrange("o (c p) k -> p (o c) k", p=P), width

        def steps(eng, step, last):
            for c in range(PEELED):
                step(Slot(0, c), None)
            with eng.Fori(0, R - 1) as k:
                for c in range(PEELED, PEELED + STEPS_A):
                    step(Slot(k, c, STEPS_A), Piece(k, c))
            with eng.Fori(0, TRIPS_B) as k:
                for c in range(LOOP_B, LOOP_B + UNROLL):
                    step(Slot(k, c), None)
            for c in range(AFTER, last):
                step(Slot(0, c), None)

        block = ctx.enter_context(nc.Block())

        @block.sync
        def _(sp):
            def load_first(m, q, r):
                src, width = source(r, m, q * QUARTER, QUARTER)
                sp.dma_start(first_staging(m, q * QUARTER, QUARTER).rearrange("p (c k) -> p c k", k=width), src
                             ).then_inc(first_loaded[m][q], DMA)

            def load_x(s):
                b = sp.value_load(seq_at[0:1, bass.ds(s.at, 1)], min_val=0, max_val=N - 1)
                return lambda: sp.dma_start(xs[:, s.buf(XRING), :], x[bass.ds(b, 1)].rearrange("o p h -> (o p) h")
                                            ).then_inc(x_loaded[s.buf(XRING)], DMA)

            def load_table(table, vector, width, rank, r, loaded):
                sp.dma_start(table[:, rank * width:(rank + 1) * width],
                             vector[bass.ds(r, 1)].partition_broadcast(P)).then_inc(loaded, DMA)

            sp.dma_start(role_in[:, :], role.rearrange("(o n) -> o n", o=1)).then_inc(roles_loaded, DMA)
            sp.wait_ge(ranked, 1)
            ids = [sp.value_load(role_by_rank[0:1, k:k + 1], min_val=0, max_val=R - 1) for k in range(R)]
            load_first(DOWN, 0, ids[0])
            load_first(DOWN, 1, ids[0])
            sp.wait_ge(sorted_ready, 1)
            load_x(Slot(0, 0))()
            load_first(DOWN, 2, ids[0])
            load_first(DOWN, 3, ids[0])
            load_x(Slot(0, 1))()
            load_table(bdown_all, b_down, K, 0, ids[0], bdown_loaded)
            load_x(Slot(0, 2))()
            for q in range(4):
                load_first(UP, q, ids[0])
            for table, vector in ((bup_all, b_up), (gamma_all, gamma), (beta_all, beta)):
                load_table(table, vector, H, 0, ids[0], tables_loaded)
            for c in range(3, XRING):
                load_x(Slot(0, c))()

            def step(s, piece):
                if s.since(3) and (s + 3).before(N):
                    load = load_x(s + 3)
                    sp.wait_ge(y_ready, (s - 3).at + 1)
                    load()
                if not s.loop and s.c < R - 1:
                    rank = s.c + 1
                    load_table(bdown_all, b_down, K, rank, ids[rank], late_tables_loaded)
                    for table, vector in ((bup_all, b_up), (gamma_all, gamma), (beta_all, beta)):
                        load_table(table, vector, H, rank, ids[rank], late_tables_loaded)
                if piece is not None and piece.phase < 2:
                    h = piece.phase
                    r = sp.value_load(role_by_rank[0:1, bass.ds(piece.k + 1, 1)], min_val=0, max_val=R - 1)
                    src, width = source(r, piece.kind, h * HALF, HALF)
                    if h == 0:
                        sp.wait_ge(wlo_ready, piece.matrix * 2 + 8)
                    sp.dma_start(stage[:, h * HALF:(h + 1) * HALF].rearrange("p (c k) -> p c k", k=width), src
                                 ).then_inc(w_loaded[h], DMA)
                if s.since(3):
                    b = sp.value_load(seq_at[0:1, bass.ds((s - 3).at, 1)], min_val=0, max_val=N - 1)
                    sp.wait_ge(result_ready, (s - 3).at + 1)
                    sp.dma_start(out[bass.ds(b, 1)].rearrange("o p h -> (o p) h"), ys[:, (s - 3).buf(YRING), :]
                                 ).then_inc(stored[(s - 3).buf(YRING)], DMA)

            steps(sp, step, N + 3)
            for j in range(YRING):
                sp.wait_ge(stored[j], DMA * len(range(j, N, YRING)))

        @block.gpsimd
        def _(pool):
            pool.iota(countdown[:, 0:N], [[-1, N]], base=N - 1, channel_multiplier=0).then_inc(countdown_ready, 1)
            pool.iota(countdown[:, N:N + R], [[-1, R]], base=R - 1, channel_multiplier=0).then_inc(countdown_ready, 1)
            pool.memset(minus_half[:, :], -0.5).then_inc(consts_ready, 1)
            pool.memset(eps[:, :], LN_EPS).then_inc(consts_ready, 1)
            pool.memset(ident[:, :], 0.0).then_inc(zeroed, 1)
            pool.wait_ge(zeroed, 1)
            pool.affine_select(out=ident[:, :], in_=ident[:, :], compare_op=ALU.not_equal, fill=1.0, base=0,
                               pattern=[[-1, P]], channel_multiplier=1).then_inc(ident_ready, 1)
            for m in (DOWN, UP):
                pool.wait_ge(fmax_ready, 4 * m + 4)
                pool.partition_all_reduce(first_all[:, m, :], first_max[:, m, :], P, ABSMAX).then_inc(fall_ready, 1)
            pool.wait_ge(sorted_ready, 1)
            pool.wait_ge(consts_ready, 2)

            def add_b_up(s):
                rank = pool.value_load(rank_at[0:1, bass.ds(s.at, 1)], min_val=0, max_val=R - 1)
                row = xs[:, s.buf(XRING), :]
                pool.wait_ge(xlo_ready, s.at + 1)
                pool.wait_ge(tables_loaded, 3 * DMA)
                pool.tensor_tensor(row, row, bup_all[:, bass.ds(rank * H, H)], ALU.add).then_inc(xres_ready, 1)

            def normalise(s):
                n = norm[:, s.buf(UNROLL), :]
                m = moments[:, s.buf(UNROLL), :]
                pool.wait_ge(moments_ready, s.at + 1)
                pool.tensor_tensor(n[:, 0:1], m[:, 1:2], eps[:, :], ALU.add).then_inc(veps_ready, 1)
                pool.tensor_scalar(n[:, 2:3], m[:, 0:1], -1.0, None, ALU.mult).then_inc(neg_ready, 1)
                pool.wait_ge(veps_ready, s.at + 1)
                pool.tensor_tensor(n[:, 1:2], n[:, 0:1], minus_half[:, :], ALU.pow).then_inc(rstd_ready, 1)
                pool.wait_ge(neg_ready, s.at + 1)
                pool.wait_ge(rstd_ready, s.at + 1)
                pool.tensor_tensor(n[:, 3:4], n[:, 2:3], n[:, 1:2], ALU.mult).then_inc(norm_ready, 1)

            def finish(s, piece):
                rank = pool.value_load(rank_at[0:1, bass.ds(s.at, 1)], min_val=0, max_val=R - 1)
                row = ys[:, s.buf(YRING), :]
                if piece is not None and piece.phase == 2:
                    pool.wait_ge(wmax_ready, piece.matrix * 2 + 2)
                pool.wait_ge(yn_ready, s.at + 1)
                pool.wait_ge(tables_loaded, 3 * DMA)
                pool.tensor_tensor(row, row, gamma_all[:, bass.ds(rank * H, H)], ALU.mult).then_inc(scaled_ready, 1)
                pool.wait_ge(scaled_ready, s.at + 1)
                pool.wait_ge(tables_loaded, 3 * DMA)
                pool.tensor_tensor(row, row, beta_all[:, bass.ds(rank * H, H)], ALU.add).then_inc(result_ready, 1)

            def step(s, piece):
                if not s.loop and s.c == PEELED - 1:
                    pool.wait_ge(late_tables_loaded, (R - 1) * 4 * DMA)
                if s.since(3):
                    normalise(s - 3)
                if s.before(N):
                    add_b_up(s)
                if s.since(3):
                    finish(s - 3, piece)
                if piece is not None and piece.phase == 2:
                    pool.partition_all_reduce(wall[:, :], wmax[:, :], P, ABSMAX).then_inc(wall_ready, 1)

            steps(pool, step, N + 3)

        @block.scalar
        def _(act):
            def split_first(m, q):
                act.wait_ge(fscale_ready, m + 1)
                act.activation(w_at(0, m, HI, q * QUARTER, QUARTER), first_staging(m, q * QUARTER, QUARTER), ACT.Copy,
                               scale=w_scale[:, m:m + 1]).then_inc(fhi_ready, 1)

            def split_later(piece, h):
                act.wait_ge(wscale_ready, piece.matrix + 1)
                act.activation(w_at(piece.k + 1, piece.kind, HI, h * HALF, HALF), stage[:, h * HALF:(h + 1) * HALF],
                               ACT.Copy, scale=w_scale[:, 2:3]).then_inc(whi_ready, 1)

            def split_x(s):
                act.wait_ge(xscale_ready, s.at + 1)
                if s.since(2):
                    act.wait_ge(xT_hi_done, s.at - 1)
                act.activation(x16[:, s.buf(2), HI, :], xs[:, s.buf(XRING), :], ACT.Copy,
                               scale=xst[:, s.buf(UNROLL), 3:4]).then_inc(xhi_ready, 1)

            def copy_xT(s):
                act.wait_ge(xT_hi_done, s.at + 1)
                if s.since(2):
                    act.wait_ge(z_done, s.at - 1)
                act.copy(xT[:, s.buf(2), HI, :, :], xT_ps[:, HI, :, :]).then_inc(xT_hi_ready, 1)
                act.wait_ge(xT_lo_done, s.at + 1)
                act.copy(xT[:, s.buf(2), LO, :, :], xT_ps[:, LO, :, :]).then_inc(xT_lo_ready, 1)

            def normalise(s):
                act.wait_ge(norm_ready, s.at + 1)
                row = ys[:, s.buf(YRING), :]
                act.activation(row, row, ACT.Identity, bias=norm[:, s.buf(UNROLL), 3:4],
                               scale=norm[:, s.buf(UNROLL), 1:2]).then_inc(yn_ready, 1)

            def gelu(s):
                act.wait_ge(z_ready, s.at + 1)
                act.activation(hs[:, s.buf(2), :], hs[:, s.buf(2), :], ACT.Gelu).then_inc(h_ready, 1)

            def copy_hT(s):
                act.wait_ge(hT_done, s.at + 1)
                if s.since(2):
                    act.wait_ge(u_done, s.at - 1)
                act.copy(hT[:, s.buf(2), :, :, :], hT_ps[:, :, :, :]).then_inc(hT_ready, 1)

            def split_h(s):
                act.wait_ge(hscale_ready, s.at + 1)
                if s.since(2):
                    act.wait_ge(hT_done, s.at - 1)
                act.activation(h16[:, s.buf(2), HI, :], hs[:, s.buf(2), :], ACT.Copy,
                               scale=hst[:, s.buf(UNROLL), 3:4]).then_inc(hhi_ready, 1)

            def step(s, piece):
                if (s + 2).before(N):
                    split_x(s + 2)
                if s.before(N):
                    gelu(s)
                if (s + 1).before(N):
                    copy_xT(s + 1)
                if s.since(3):
                    normalise(s - 3)
                if s.before(N):
                    split_h(s)
                if s.since(1) and (s - 1).before(N):
                    copy_hT(s - 1)
                if piece is not None and piece.phase in (3, 4):
                    split_later(piece, piece.phase - 3)
                if not s.loop and s.c == 0:
                    for q in range(4):
                        split_first(UP, q)

            split_x(Slot(0, 0))
            split_first(DOWN, 0)
            copy_xT(Slot(0, 0))
            for q in range(1, 4):
                split_first(DOWN, q)
            split_x(Slot(0, 1))
            steps(act, step, N + 3)

        @block.vector
        def _(dve):
            chained = [0]

            def link(ins):
                chained[0] += 1
                ins.then_inc(chain, 1)
                dve.wait_ge(chain, chained[0])

            def rank_roles():
                n, key, r0, r1, rank = (per_role[:, i, :] for i in range(5))
                dve.wait_ge(countdown_ready, 2)
                link(dve.tensor_copy(countdown_f[:, :], countdown[:, :]))
                rev_seq, rev_role = countdown_f[:, 0:N], countdown_f[:, N:N + R]
                dve.wait_ge(roles_loaded, DMA)
                link(dve.tensor_scalar(role_f[:, 0, :], role_in[:, :], 0.0, float(R), ALU.is_lt, ALU.mult))
                link(dve.tensor_tensor(role_f[:, 1, :], role_in[:, :], role_f[:, 0, :], ALU.add))
                link(dve.tensor_scalar(role_f[:, 2, :], role_f[:, 1, :], 0.0, float(R - 1), ALU.max, ALU.min))
                for r in range(R):
                    link(dve.tensor_scalar(is_role[:, r, :], role_f[:, 2, :], float(r), None, ALU.is_equal))
                link(dve.tensor_reduce(n, is_role[:, :, :], AX_X, ALU.add))
                link(dve.scalar_tensor_tensor(out=key, in0=n, scalar=float(R), in1=rev_role, op0=ALU.mult, op1=ALU.add))
                link(dve.tensor_scalar(r0, key, key[:, 0:1], None, ALU.is_lt))
                link(dve.scalar_tensor_tensor(out=r1, in0=key, scalar=key[:, 1:2], in1=r0, op0=ALU.is_lt, op1=ALU.add))
                link(dve.scalar_tensor_tensor(out=rank, in0=key, scalar=key[:, 2:3], in1=r1, op0=ALU.is_lt, op1=ALU.add))
                for k in range(R):
                    link(dve.scalar_tensor_tensor(out=picks[:, k, :], in0=rank, scalar=float(k), in1=rev_role,
                                                  op0=ALU.is_equal, op1=ALU.mult))
                link(dve.tensor_reduce(picked[:, :], picks[:, :, :], AX_X, ALU.add))
                dve.tensor_scalar(role_by_rank[:, :], picked[:, :], -1.0, float(R - 1), ALU.mult, ALU.add
                                  ).then_inc(ranked, 1)
                return rank, rev_seq

            def sort_sequences(rank, rev_seq):
                link(dve.tensor_scalar(rank_of[:, 0, :], is_role[:, 0, :], rank[:, 0:1], None, ALU.mult))
                for r in (1, 2):
                    link(dve.scalar_tensor_tensor(out=rank_of[:, r, :], in0=is_role[:, r, :], scalar=rank[:, r:r + 1],
                                                  in1=rank_of[:, r - 1, :], op0=ALU.mult, op1=ALU.add))
                link(dve.scalar_tensor_tensor(out=keys[:, 0, :], in0=rank_of[:, 2, :], scalar=float(-N), in1=rev_seq,
                                              op0=ALU.mult, op1=ALU.add))
                for g in range(N // 8):
                    top = order_f[:, 0, 8 * g:8 * g + 8]
                    link(dve.max(top, keys[:, g % 2, :]))
                    if g + 1 < N // 8:
                        link(dve.match_replace(keys[:, (g + 1) % 2, :], top, keys[:, g % 2, :], -1e9))
                key, r0, rank_s = (order_f[:, i, :] for i in range(3))
                link(dve.tensor_scalar(r0, key, 0.0, None, ALU.is_lt))
                link(dve.scalar_tensor_tensor(out=rank_s, in0=key, scalar=float(-N), in1=r0, op0=ALU.is_lt, op1=ALU.add))
                link(dve.tensor_copy(rank_at[:, :], rank_s))
                link(dve.scalar_tensor_tensor(out=r0, in0=rank_s, scalar=float(-N), in1=key, op0=ALU.mult,
                                              op1=ALU.subtract))
                dve.tensor_scalar(seq_at[:, :], r0, float(N - 1), None, ALU.add).then_inc(sorted_ready, 1)

            def power_scales(count, top, power, inverse, scale, pow_ready, inv_ready, scale_ready):
                dve.tensor_scalar(power.bitcast(I32), top.bitcast(I32), EXPONENT_BITS, None, ALU.bitwise_and
                                  ).then_inc(pow_ready, 1)
                dve.wait_ge(pow_ready, count)
                dve.tensor_scalar(inverse, power, TINIEST, 1.0 / TOP, ALU.max, ALU.mult).then_inc(inv_ready, 1)
                dve.wait_ge(inv_ready, count)
                dve.reciprocal(scale, inverse).then_inc(scale_ready, 1)

            def largest_first(m, q):
                dve.wait_ge(first_loaded[m][q], DMA)
                dve.tensor_reduce(first_max[:, m, q:q + 1], first_staging(m, q * QUARTER, QUARTER), AX_X, ALU.max,
                                  apply_absolute_value=True).then_inc(fmax_ready, 1)

            def scale_first(m):
                dve.wait_ge(fall_ready, m + 1)
                dve.tensor_reduce(wpow[:, 0:1], first_all[:, m, :], AX_X, ALU.max).then_inc(ftop_ready, 1)
                dve.wait_ge(ftop_ready, m + 1)
                power_scales(m + 1, wpow[:, 0:1], wpow[:, 1:2], w_inv[:, m:m + 1], w_scale[:, m:m + 1],
                             fpow_ready, finv_ready, fscale_ready)

            def split_first(m, q):
                dve.wait_ge(fhi_ready, 4 * m + q + 1)
                dve.scalar_tensor_tensor(out=w_at(0, m, LO, q * QUARTER, QUARTER),
                                         in0=first_staging(m, q * QUARTER, QUARTER), scalar=w_scale[:, m:m + 1],
                                         in1=w_at(0, m, HI, q * QUARTER, QUARTER), op0=ALU.mult, op1=ALU.subtract
                                         ).then_inc(wlo_ready, 1)

            def largest_later(piece, h):
                dve.wait_ge(w_loaded[h], piece.matrix * DMA + DMA)
                dve.tensor_reduce(wmax[:, h:h + 1], stage[:, h * HALF:(h + 1) * HALF], AX_X, ALU.max,
                                  apply_absolute_value=True).then_inc(wmax_ready, 1)

            def scale_later(piece):
                dve.wait_ge(wall_ready, piece.matrix + 1)
                dve.tensor_reduce(wpow[:, 0:1], wall[:, :], AX_X, ALU.max).then_inc(wtop_ready, 1)
                dve.wait_ge(wtop_ready, piece.matrix + 1)
                power_scales(piece.matrix + 1, wpow[:, 0:1], wpow[:, 1:2], wpow[:, 2:3], w_scale[:, 2:3],
                             wpow_ready, winv_ready, wscale_ready)
                dve.tensor_copy(w_inv[:, bass.ds(piece.matrix + 2, 1)], wpow[:, 2:3]).then_inc(wtable_ready, 1)

            def split_later(piece, h):
                dve.wait_ge(whi_ready, piece.matrix * 2 + h + 1)
                dve.scalar_tensor_tensor(out=w_at(piece.k + 1, piece.kind, LO, h * HALF, HALF),
                                         in0=stage[:, h * HALF:(h + 1) * HALF], scalar=w_scale[:, 2:3],
                                         in1=w_at(piece.k + 1, piece.kind, HI, h * HALF, HALF),
                                         op0=ALU.mult, op1=ALU.subtract).then_inc(wlo_ready, 1)

            def largest_x(s):
                dve.wait_ge(x_loaded[s.buf(XRING)], s.turn(XRING) * DMA + DMA)
                dve.tensor_reduce(xst[:, s.buf(UNROLL), 0:1], xs[:, s.buf(XRING), :], AX_X, ALU.max,
                                  apply_absolute_value=True).then_inc(xmax_ready, 1)

            def scale_x(s):
                st = xst[:, s.buf(UNROLL), :]
                dve.wait_ge(xmax_ready, s.at + 1)
                power_scales(s.at + 1, st[:, 0:1], st[:, 1:2], st[:, 2:3], st[:, 3:4],
                             xpow_ready, xinv_ready, xscale_ready)

            def split_x(s):
                dve.wait_ge(xhi_ready, s.at + 1)
                if s.since(2):
                    dve.wait_ge(xT_lo_done, s.at - 1)
                dve.scalar_tensor_tensor(out=x16[:, s.buf(2), LO, :], in0=xs[:, s.buf(XRING), :],
                                         scalar=xst[:, s.buf(UNROLL), 3:4], in1=x16[:, s.buf(2), HI, :],
                                         op0=ALU.mult, op1=ALU.subtract).then_inc(xlo_ready, 1)

            def make_z(s):
                rank = dve.value_load(rank_at[0:1, bass.ds(s.at, 1)], min_val=0, max_val=R - 1)
                j = s.buf(UNROLL)
                dve.tensor_tensor(undo[:, j, 0:1], xst[:, j, 2:3], w_inv[:, bass.ds(rank * 2 + DOWN, 1)], ALU.mult
                                  ).then_inc(zundo_ready, 1)
                dve.wait_ge(zundo_ready, s.at + 1)
                if s.since(2):
                    dve.wait_ge(hhi_ready, s.at - 1)
                dve.wait_ge(z_done, s.at + 1)
                dve.scalar_tensor_tensor(out=hs[:, s.buf(2), :], in0=z_ps[:, s.buf(2), :], scalar=undo[:, j, 0:1],
                                         in1=bdown_all[:, bass.ds(rank * K, K)], op0=ALU.mult, op1=ALU.add
                                         ).then_inc(z_ready, 1)

            def scale_h(s):
                j = s.buf(UNROLL)
                dve.wait_ge(h_ready, s.at + 1)
                dve.tensor_reduce(hst[:, j, 0:1], hs[:, s.buf(2), :], AX_X, ALU.max, apply_absolute_value=True
                                  ).then_inc(hmax_ready, 1)
                dve.wait_ge(hmax_ready, s.at + 1)
                power_scales(s.at + 1, hst[:, j, 0:1], hst[:, j, 1:2], hst[:, j, 2:3], hst[:, j, 3:4],
                             hpow_ready, hinv_ready, hscale_ready)

            def split_h(s):
                dve.wait_ge(hhi_ready, s.at + 1)
                dve.scalar_tensor_tensor(out=h16[:, s.buf(2), LO, :], in0=hs[:, s.buf(2), :],
                                         scalar=hst[:, s.buf(UNROLL), 3:4], in1=h16[:, s.buf(2), HI, :],
                                         op0=ALU.mult, op1=ALU.subtract).then_inc(hlo_ready, 1)

            def make_y(s):
                rank = dve.value_load(rank_at[0:1, bass.ds(s.at, 1)], min_val=0, max_val=R - 1)
                j = s.buf(UNROLL)
                dve.tensor_tensor(undo[:, j, 1:2], hst[:, j, 2:3], w_inv[:, bass.ds(rank * 2 + UP, 1)], ALU.mult
                                  ).then_inc(uundo_ready, 1)
                dve.wait_ge(uundo_ready, s.at + 1)
                dve.wait_ge(u_done, s.at + 1)
                dve.wait_ge(xres_ready, s.at + 1)
                if s.since(YRING):
                    dve.wait_ge(stored[s.buf(YRING)], s.turn(YRING) * DMA)
                dve.scalar_tensor_tensor(out=ys[:, s.buf(YRING), :], in0=u_ps[:, :],
                                         scalar=undo[:, j, 1:2], in1=xs[:, s.buf(XRING), :],
                                         op0=ALU.mult, op1=ALU.add).then_inc(y_ready, 1)
                dve.wait_ge(y_ready, s.at + 1)
                for c in range(H // BANK):
                    dve.bn_stats(stats[:, j, c, :], ys[:, s.buf(YRING), c * BANK:(c + 1) * BANK]
                                 ).then_inc(stats_ready, 1)

            def make_moments(s):
                j = s.buf(UNROLL)
                dve.bn_aggr(moments[:, j, :], stats[:, j, :, :]).then_inc(moments_ready, 1)

            def step(s, piece):
                if not s.loop and s.c == PEELED - 1:
                    dve.wait_ge(late_tables_loaded, (R - 1) * 4 * DMA)
                if s.since(3):
                    make_y(s - 3)
                if s.since(1) and (s - 1).before(N):
                    split_h(s - 1)
                if s.since(3):
                    dve.wait_ge(stats_ready, (s - 3).at * 2 + 2)
                if (s + 2).before(N):
                    largest_x(s + 2)
                if s.since(3):
                    make_moments(s - 3)
                if (s + 2).before(N):
                    scale_x(s + 2)
                if piece is not None and piece.phase == 3:
                    scale_later(piece)
                if s.before(N):
                    make_z(s)
                if piece is not None and piece.phase in (1, 2):
                    largest_later(piece, piece.phase - 1)
                if (s + 2).before(N):
                    split_x(s + 2)
                if s.before(N):
                    scale_h(s)
                if piece is not None and piece.phase in (4, 5):
                    split_later(piece, piece.phase - 4)
                if not s.loop and s.c == 0:
                    scale_first(UP)
                    for q in range(4):
                        split_first(UP, q)

            rank, rev_seq = rank_roles()
            sort_sequences(rank, rev_seq)
            largest_first(DOWN, 0)
            largest_first(DOWN, 1)
            largest_x(Slot(0, 0))
            scale_x(Slot(0, 0))
            largest_first(DOWN, 2)
            largest_first(DOWN, 3)
            split_x(Slot(0, 0))
            scale_first(DOWN)
            largest_x(Slot(0, 1))
            scale_x(Slot(0, 1))
            for q in range(4):
                split_first(DOWN, q)
            split_x(Slot(0, 1))
            for q in range(4):
                largest_first(UP, q)
            dve.wait_ge(bdown_loaded, DMA)
            steps(dve, step, N + 3)

        @block.tensor
        def _(pe):
            pe.wait_ge(ident_ready, 1)
            pe.wait_ge(sorted_ready, 1)

            def transpose_x(s):
                for part, taken, copied, done in ((HI, xhi_ready, xT_hi_ready, xT_hi_done),
                                                  (LO, xlo_ready, xT_lo_ready, xT_lo_done)):
                    pe.wait_ge(taken, s.at + 1)
                    if s.since(1):
                        pe.wait_ge(copied, s.at)
                    for c in range(HC):
                        t = pe.transpose(xT_ps[:, part, c, :], x16[:, s.buf(2), part, c * P:(c + 1) * P], ident[:, :])
                    t.then_inc(done, 1)

            def transpose_h(s):
                pe.wait_ge(hlo_ready, s.at + 1)
                if s.since(1):
                    pe.wait_ge(hT_ready, s.at)
                for part in (HI, LO):
                    for c in range(KC):
                        t = pe.transpose(hT_ps[:, part, c, :], h16[:, s.buf(2), part, c * P:(c + 1) * P], ident[:, :])
                t.then_inc(hT_done, 1)

            def down(s):
                rank = pe.value_load(rank_at[0:1, bass.ds(s.at, 1)], min_val=0, max_val=R - 1)
                if s.since(2):
                    pe.wait_ge(z_ready, s.at - 1)
                pe.wait_ge(xT_lo_ready, s.at + 1)
                for c in range(HC):
                    if not s.loop and s.c == 0 and c % 2 == 0:
                        pe.wait_ge(wlo_ready, c // 2 + 1)
                    for a, w in ((HI, HI), (HI, LO), (LO, HI)):
                        t = pe.matmul(z_ps[:, s.buf(2), :], xT[:, s.buf(2), a, c, :], w_at(rank, DOWN, w, c * K, K),
                                      start=(c == 0 and a == HI and w == HI), stop=(c == HC - 1 and a == LO))
                t.then_inc(z_done, 1)

            def up(s):
                rank = pe.value_load(rank_at[0:1, bass.ds(s.at, 1)], min_val=0, max_val=R - 1)
                if s.since(1):
                    pe.wait_ge(y_ready, s.at)
                pe.wait_ge(hT_ready, s.at + 1)
                for c in range(KC):
                    if not s.loop and s.c == 0:
                        pe.wait_ge(wlo_ready, 4 + c + 1)
                    for a, w in ((HI, HI), (HI, LO), (LO, HI)):
                        for n in range(H // BANK):
                            t = pe.matmul(u_ps[:, n * BANK:(n + 1) * BANK], hT[:, s.buf(2), a, c, :],
                                          w_at(rank, UP, w, c * H + n * BANK, BANK),
                                          start=(c == 0 and a == HI and w == HI), stop=(c == KC - 1 and a == LO))
                t.then_inc(u_done, 1)

            def step(s, piece):
                if piece is not None and piece.kind == UP and piece.phase == 0:
                    pe.wait_ge(wlo_ready, piece.k * 4 + 8)
                if s.loop and piece is None and s.c == LOOP_B + UNROLL - 1:
                    pe.wait_ge(wlo_ready, 8 + 4 * (R - 1))
                if s.before(N):
                    down(s)
                if s.since(1) and (s - 1).before(N):
                    transpose_h(s - 1)
                if (s + 1).before(N):
                    transpose_x(s + 1)
                if s.since(2):
                    up(s - 2)

            transpose_x(Slot(0, 0))
            steps(pe, step, N + 2)


_INS = ["x", "itok_B_1_2", "L0_cond_W_down", "L0_cond_b_down", "L0_cond_W_up", "L0_cond_b_up",
        "L0_cond_gamma", "L0_cond_beta"]
_OUT = ((64, 128, 1024), "float32")


def kernel(**inputs):
    import numpy as _np
    import concourse.bacc as _bacc
    from concourse import mybir as _mybir
    from concourse.bass_utils import run_bass_kernel_spmd as _run

    nc = _bacc.Bacc("TRN2", target_bir_lowering=False, num_devices=1,
                    dynamic_dma_scratch_size=1024)
    arrays, args = {}, []
    for name in _INS:
        a = _np.ascontiguousarray(inputs[name])
        arrays[f"in_{name}_dram"] = a
        args.append(nc.dram_tensor(f"in_{name}_dram", a.shape, _mybir.dt.from_np(a.dtype), kind="ExternalInput").ap())
    shape, dtype = _OUT
    args.append(nc.dram_tensor("out_0_dram", shape, _mybir.dt.from_np(_np.dtype(dtype)), kind="ExternalOutput").ap())
    adapter(nc, *args)
    r = _run(nc, [arrays], core_ids=[0])
    return r.results[0]["out_0_dram"]
```

```python
from contextlib import ExitStack

import concourse.bass as bass
from concourse import mybir
from concourse.alu_op_type import AluOpType as ALU

F32 = mybir.dt.float32
F16 = mybir.dt.float16
I32 = mybir.dt.int32
ACT = mybir.ActivationFunctionType
AX_X = mybir.AxisListType.X
ABSMAX = bass.bass_isa.ReduceOp.absmax

P = 128
HI, LO = 0, 1
PASSES = ((HI, HI), (HI, LO), (LO, HI))
DOWN, UP = 0, 1
LN_EPS = 1e-5
EXPONENT_BITS = 0x7F800000
TINIEST = 2.0 ** -100
TOP = 2.0 ** 14
DMA = 16
UNROLL = 6
PEELED = 4


class Slot:

    def __init__(self, k, c, stride=UNROLL):
        self.k, self.c, self.stride, self.loop = k, c, stride, not isinstance(k, int)
        self.at = k * stride + c

    def __add__(self, d):
        return Slot(self.k, self.c + d, self.stride)

    def __sub__(self, d):
        return Slot(self.k, self.c - d, self.stride)

    def since(self, first):
        return self.loop or self.c >= first

    def before(self, end):
        return self.loop or self.c < end

    def buf(self, ring):
        return self.c % ring

    def turn(self, ring):
        return self.k * (self.stride // ring) + self.c // ring


class Piece:

    def __init__(self, k, c):
        self.k, self.kind, self.phase = k, (c - PEELED) // UNROLL, (c - PEELED) % UNROLL
        self.matrix = k * 2 + self.kind


def adapter(nc, x, role, w_down, b_down, w_up, b_up, gamma, beta, out):
    N, S, H = x.shape
    R, _, K = w_down.shape
    HC, KC = H // P, K // P
    WSIZE = H * K // P
    QUARTER, HALF = WSIZE // 4, WSIZE // 2
    BANK = 512
    XRING, YRING = 6, 3
    FIRST = 6
    STEPS_A = 2 * UNROLL
    LOOP_B = PEELED + (R - 1) * STEPS_A
    TRIPS_B = (N - XRING - LOOP_B) // UNROLL
    AFTER = LOOP_B + TRIPS_B * UNROLL
    assert S == P and K == BANK and H == 2 * BANK and R == 3 and N % 8 == 0 and N & (N - 1) == 0
    assert PEELED + STEPS_A + UNROLL <= -(-N // R) and LOOP_B + UNROLL <= -(-2 * N // R)

    with ExitStack() as ctx:
        def sb(name, shape, dt):
            return ctx.enter_context(nc.sbuf_tensor(name, shape, dt))

        def psum(name, shape, dt):
            return ctx.enter_context(nc.psum_tensor(name, shape, dt))

        def sem(name):
            return ctx.enter_context(nc.semaphore(name))

        weights = sb("weights", [P, R * 2 * 2 * WSIZE], F16)
        stage = sb("stage", [P, WSIZE], F32)
        bdown_all = sb("bdown_all", [P, R * K], F32)
        bup_all = sb("bup_all", [P, R * H], F32)
        gamma_all = sb("gamma_all", [P, R * H], F32)
        beta_all = sb("beta_all", [P, R * H], F32)
        xs = sb("xs", [P, XRING, H], F32)
        x16 = sb("x16", [P, 2, 2, H], F16)
        xT = sb("xT", [P, 2, 2, HC, P], F16)
        hs = sb("hs", [P, 2, K], F32)
        h16 = sb("h16", [P, 2, 2, K], F16)
        hT = sb("hT", [P, 2, 2, KC, P], F16)
        ys = sb("ys", [P, YRING, H], F32)
        ident = sb("ident", [P, P], F16)

        carved = [0]

        def carve(*dims):
            at, size = carved[0], 1
            for d in dims:
                size *= d
            carved[0] = at + size
            assert carved[0] <= 2 * K
            flat = hs[0:1, :, :].rearrange("o a k -> o (a k)")[:, at:at + size]
            return flat.rearrange("o (a n) -> o a n", a=dims[0]) if len(dims) == 2 else flat

        role_in = sb("role_in", [1, N], I32)
        counting = sb("counting", [1, N + R], I32)
        counting_f = carve(N + R)
        role_f = carve(3, N)
        is_role = carve(R, N)
        per_role = carve(R)
        role_keys = carve(2, 8)
        keys = carve(4, N)
        sorted_keys = carve(2, N)
        top_role = sb("top_role", [1, R], I32)
        top_seq = sb("top_seq", [1, N], I32)
        role_by_rank = sb("role_by_rank", [1, R], I32)
        rank_at = sb("rank_at", [1, N], I32)
        seq_at = sb("seq_at", [1, N], I32)

        first_max = sb("first_max", [P, 2, 4], F32)
        first_all = sb("first_all", [P, 2, 4], F32)
        wmax = sb("wmax", [P, 2], F32)
        wall = sb("wall", [P, 2], F32)
        wpow = sb("wpow", [P, 3], F32)
        w_scale = sb("w_scale", [P, 3], F32)
        w_inv = sb("w_inv", [P, 2 * R], F32)
        xst = sb("xst", [P, UNROLL, 4], F32)
        hst = sb("hst", [P, UNROLL, 4], F32)
        undo = sb("undo", [P, UNROLL, 2], F32)
        stats = sb("stats", [P, UNROLL, 2, 6], F32)
        moments = sb("moments", [P, UNROLL, 2], F32)
        norm = sb("norm", [P, UNROLL, 4], F32)
        minus_half = sb("minus_half", [P, 1], F32)
        eps = sb("eps", [P, 1], F32)
        warm = sb("warm", [P, 1], F32)

        z_ps = psum("z_ps", [P, 2, K], F32)
        u_ps = psum("u_ps", [P, H], F32)
        xT_ps = psum("xT_ps", [P, 2, HC, P], F16)
        hT_ps = psum("hT_ps", [P, 2, KC, P], F16)

        roles_loaded, chain, consts_ready = sem("roles_loaded"), sem("chain"), sem("consts_ready")
        counting_ready, ranked, sorted_ready = sem("counting_ready"), sem("ranked"), sem("sorted_ready")
        zeroed, ident_ready = sem("zeroed"), sem("ident_ready")
        bdown_loaded, tables_loaded, late_tables_loaded = (
            sem("bdown_loaded"), sem("tables_loaded"), sem("late_tables_loaded"))
        first_loaded = [[sem(f"first_loaded{m}{q}") for q in range(4)] for m in (DOWN, UP)]
        fmax_ready, fall_ready, ftop_ready = sem("fmax_ready"), sem("fall_ready"), sem("ftop_ready")
        fpow_ready, finv_ready, fscale_ready = sem("fpow_ready"), sem("finv_ready"), sem("fscale_ready")
        fhi_ready = sem("fhi_ready")
        up_scaled, up_lo_ready = sem("up_scaled"), sem("up_lo_ready")
        w_loaded = [sem(f"w_loaded{h}") for h in range(2)]
        wmax_ready, wall_ready, wtop_ready = sem("wmax_ready"), sem("wall_ready"), sem("wtop_ready")
        wpow_ready, winv_ready, wscale_ready = sem("wpow_ready"), sem("winv_ready"), sem("wscale_ready")
        whi_ready, wtable_ready = sem("whi_ready"), sem("wtable_ready")
        wlo_ready = sem("wlo_ready")
        x_loaded = [sem(f"x_loaded{j}") for j in range(XRING)]
        xmax_ready, xpow_ready, xinv_ready = sem("xmax_ready"), sem("xpow_ready"), sem("xinv_ready")
        xscale_ready, xhi_ready, xlo_ready = sem("xscale_ready"), sem("xhi_ready"), sem("xlo_ready")
        xres_ready = sem("xres_ready")
        xT_hi_done, xT_lo_done = sem("xT_hi_done"), sem("xT_lo_done")
        xT_hi_ready, xT_lo_ready = sem("xT_hi_ready"), sem("xT_lo_ready")
        z_done, zundo_ready, z_ready, h_ready = sem("z_done"), sem("zundo_ready"), sem("z_ready"), sem("h_ready")
        hmax_ready, hpow_ready, hinv_ready = sem("hmax_ready"), sem("hpow_ready"), sem("hinv_ready")
        hscale_ready, hhi_ready, hlo_ready = sem("hscale_ready"), sem("hhi_ready"), sem("hlo_ready")
        hT_done, hT_ready = sem("hT_done"), sem("hT_ready")
        u_done, uundo_ready, y_ready = sem("u_done"), sem("uundo_ready"), sem("y_ready")
        stats_ready, moments_ready = sem("stats_ready"), sem("moments_ready")
        veps_ready, neg_ready, rstd_ready = sem("veps_ready"), sem("neg_ready"), sem("rstd_ready")
        norm_ready = sem("norm_ready")
        yn_ready, scaled_ready, result_ready = sem("yn_ready"), sem("scaled_ready"), sem("result_ready")
        last_u_done, last_y_ready = sem("last_u_done"), sem("last_y_ready")
        last_scaled, last_result_ready = sem("last_scaled"), sem("last_result_ready")
        stored = [sem(f"stored{j}") for j in range(YRING)]

        def w_at(rank, m, part, first, count):
            return weights[:, bass.ds(rank * (4 * WSIZE) + ((2 * m + part) * WSIZE + first), count)]

        def u_banks(s):
            return z_ps[:, :, :].rearrange("p a k -> p (a k)") if not s.loop and s.c == N - 2 else u_ps[:, :]

        def first_staging(m, first, count):
            if m == DOWN:
                return stage[:, first:first + count]
            at = ((R - 1) * 2 + UP) * 2 * WSIZE
            return weights[:, at:at + 2 * WSIZE].bitcast(F32)[:, first:first + count]

        def source(r, m, first, count):
            w, width = ((w_down, K), (w_up, H))[m]
            rows = w[bass.ds(r, 1), first // width * P:(first + count) // width * P, :]
            return rows.rearrange("o (c p) k -> p (o c) k", p=P), width

        def steps(eng, step, last):
            for c in range(PEELED):
                step(Slot(0, c), None)
            with eng.Fori(0, R - 1) as k:
                for c in range(PEELED, PEELED + STEPS_A):
                    step(Slot(k, c, STEPS_A), Piece(k, c))
            with eng.Fori(0, TRIPS_B) as k:
                for c in range(LOOP_B, LOOP_B + UNROLL):
                    step(Slot(k, c), None)
            for c in range(AFTER, last):
                step(Slot(0, c), None)

        block = ctx.enter_context(nc.Block())

        @block.sync
        def _(sp):
            def load_first(m, q, r):
                src, width = source(r, m, q * QUARTER, QUARTER)
                sp.dma_start(first_staging(m, q * QUARTER, QUARTER).rearrange("p (c k) -> p c k", k=width), src
                             ).then_inc(first_loaded[m][q], DMA)

            def load_x(s):
                b = sp.value_load(seq_at[0:1, bass.ds(s.at, 1)], min_val=0, max_val=N - 1)
                return lambda: sp.dma_start(xs[:, s.buf(XRING), :], x[bass.ds(b, 1)].rearrange("o p h -> (o p) h")
                                            ).then_inc(x_loaded[s.buf(XRING)], DMA)

            def store(s):
                b = sp.value_load(seq_at[0:1, bass.ds(s.at, 1)], min_val=0, max_val=N - 1)
                if s.before(N - 2):
                    sp.wait_ge(result_ready, s.at + 1)
                    sp.dma_start(out[bass.ds(b, 1)].rearrange("o p h -> (o p) h"), ys[:, s.buf(YRING), :]
                                 ).then_inc(stored[s.buf(YRING)], DMA)
                    return
                for c in range(2):
                    cols = slice(c * BANK, (c + 1) * BANK)
                    sp.wait_ge(last_result_ready, (s.c - (N - 2)) * 2 + c + 1)
                    sp.dma_start(out[bass.ds(b, 1), :, cols].rearrange("o p h -> (o p) h"), ys[:, s.buf(YRING), cols]
                                 ).then_inc(stored[s.buf(YRING)], DMA)

            def load_table(table, vector, width, rank, r, loaded):
                sp.dma_start(table[:, rank * width:(rank + 1) * width],
                             vector[bass.ds(r, 1)].partition_broadcast(P)).then_inc(loaded, DMA)

            sp.dma_start(role_in[:, :], role.rearrange("(o n) -> o n", o=1)).then_inc(roles_loaded, DMA)
            sp.wait_ge(ranked, 1)
            ids = [sp.value_load(role_by_rank[0:1, 0:1], min_val=0, max_val=R - 1)]
            for q in range(4):
                load_first(DOWN, q, ids[0])
            ids += [sp.value_load(role_by_rank[0:1, k:k + 1], min_val=0, max_val=R - 1) for k in range(1, R)]
            sp.wait_ge(sorted_ready, 1)
            load_x(Slot(0, 0))()
            load_x(Slot(0, 1))()
            load_table(bdown_all, b_down, K, 0, ids[0], bdown_loaded)
            load_x(Slot(0, 2))()
            for q in range(4):
                load_first(UP, q, ids[0])
            for table, vector in ((bup_all, b_up), (gamma_all, gamma), (beta_all, beta)):
                load_table(table, vector, H, 0, ids[0], tables_loaded)
            for c in range(3, XRING):
                load_x(Slot(0, c))()

            def step(s, piece):
                if s.since(3) and (s + 3).before(N):
                    load = load_x(s + 3)
                    sp.wait_ge(y_ready, (s - 3).at + 1)
                    load()
                if not s.loop and s.c < R - 1:
                    rank = s.c + 1
                    load_table(bdown_all, b_down, K, rank, ids[rank], late_tables_loaded)
                    for table, vector in ((bup_all, b_up), (gamma_all, gamma), (beta_all, beta)):
                        load_table(table, vector, H, rank, ids[rank], late_tables_loaded)
                if piece is not None and piece.phase < 2:
                    h = piece.phase
                    r = sp.value_load(role_by_rank[0:1, bass.ds(piece.k + 1, 1)], min_val=0, max_val=R - 1)
                    src, width = source(r, piece.kind, h * HALF, HALF)
                    if h == 0:
                        sp.wait_ge(wlo_ready, piece.matrix * 2 + FIRST)
                    sp.dma_start(stage[:, h * HALF:(h + 1) * HALF].rearrange("p (c k) -> p c k", k=width), src
                                 ).then_inc(w_loaded[h], DMA)
                if s.since(3):
                    store(s - 3)

            steps(sp, step, N + 3)
            for j in range(YRING):
                halved = len([c for c in (N - 2, N - 1) if c % YRING == j])
                sp.wait_ge(stored[j], DMA * (len(range(j, N, YRING)) + halved))

        @block.gpsimd
        def _(pool):
            pool.iota(counting[:, 0:N], [[1, N]], base=0, channel_multiplier=0).then_inc(counting_ready, 1)
            pool.iota(counting[:, N:N + R], [[N, R]], base=0, channel_multiplier=0).then_inc(counting_ready, 1)
            pool.memset(minus_half[:, :], -0.5).then_inc(consts_ready, 1)
            pool.memset(eps[:, :], LN_EPS).then_inc(consts_ready, 1)
            pool.memset(ident[:, :], 0.0).then_inc(zeroed, 1)
            pool.wait_ge(zeroed, 1)
            pool.affine_select(out=ident[:, :], in_=ident[:, :], compare_op=ALU.not_equal, fill=1.0, base=0,
                               pattern=[[-1, P]], channel_multiplier=1).then_inc(ident_ready, 1)
            pool.wait_ge(fmax_ready, 4)
            pool.partition_all_reduce(first_all[:, DOWN, :], first_max[:, DOWN, :], P, ABSMAX).then_inc(fall_ready, 1)

            def add_b_up(s):
                rank = pool.value_load(rank_at[0:1, bass.ds(s.at, 1)], min_val=0, max_val=R - 1)
                row = xs[:, s.buf(XRING), :]
                pool.wait_ge(xlo_ready, s.at + 1)
                pool.wait_ge(tables_loaded, 3 * DMA)
                pool.tensor_tensor(row, row, bup_all[:, bass.ds(rank * H, H)], ALU.add).then_inc(xres_ready, 1)

            def normalise(s):
                n = norm[:, s.buf(UNROLL), :]
                m = moments[:, s.buf(UNROLL), :]
                pool.wait_ge(moments_ready, s.at + 1)
                pool.tensor_tensor(n[:, 0:1], m[:, 1:2], eps[:, :], ALU.add).then_inc(veps_ready, 1)
                if s.before(N - 2):
                    pool.tensor_scalar(n[:, 2:3], m[:, 0:1], -1.0, None, ALU.mult).then_inc(neg_ready, 1)
                pool.wait_ge(veps_ready, s.at + 1)
                pool.tensor_tensor(n[:, 1:2], n[:, 0:1], minus_half[:, :], ALU.pow).then_inc(rstd_ready, 1)
                if not s.before(N - 2):
                    return
                pool.wait_ge(neg_ready, s.at + 1)
                pool.wait_ge(rstd_ready, s.at + 1)
                pool.tensor_tensor(n[:, 3:4], n[:, 2:3], n[:, 1:2], ALU.mult).then_inc(norm_ready, 1)

            def finish(s, piece):
                rank = pool.value_load(rank_at[0:1, bass.ds(s.at, 1)], min_val=0, max_val=R - 1)
                row = ys[:, s.buf(YRING), :]
                if piece is not None and piece.phase == 2:
                    pool.wait_ge(wmax_ready, piece.matrix * 2 + 2)
                pool.wait_ge(yn_ready, s.at + 1)
                pool.wait_ge(tables_loaded, 3 * DMA)
                pool.tensor_tensor(row, row, gamma_all[:, bass.ds(rank * H, H)], ALU.mult).then_inc(scaled_ready, 1)
                pool.wait_ge(scaled_ready, s.at + 1)
                pool.wait_ge(tables_loaded, 3 * DMA)
                pool.tensor_tensor(row, row, beta_all[:, bass.ds(rank * H, H)], ALU.add).then_inc(result_ready, 1)

            def step(s, piece):
                if not s.loop and s.c == 0:
                    add_b_up(s)
                    pool.wait_ge(fmax_ready, 4 + 4)
                    pool.partition_all_reduce(first_all[:, UP, :], first_max[:, UP, :], P, ABSMAX
                                              ).then_inc(fall_ready, 1)
                    return
                if not s.loop and s.c == 1:
                    for q in (2, 3):
                        pool.wait_ge(fhi_ready, 4 + q + 1)
                        pool.tensor_tensor(w_at(0, UP, LO, q * QUARTER, QUARTER),
                                           first_staging(UP, q * QUARTER, QUARTER),
                                           w_at(0, UP, HI, q * QUARTER, QUARTER), ALU.subtract).then_inc(up_lo_ready, 1)
                if not s.loop and s.c == PEELED - 1:
                    pool.wait_ge(late_tables_loaded, (R - 1) * 4 * DMA)
                if s.since(3):
                    normalise(s - 3)
                if s.before(N):
                    add_b_up(s)
                if s.since(3) and (s - 3).before(N - 2):
                    finish(s - 3, piece)
                if piece is not None and piece.phase == 2:
                    pool.partition_all_reduce(wall[:, :], wmax[:, :], P, ABSMAX).then_inc(wall_ready, 1)

            steps(pool, step, N + 3)

        @block.scalar
        def _(act):
            def split_first(m, q):
                act.wait_ge(fscale_ready, m + 1)
                act.activation(w_at(0, m, HI, q * QUARTER, QUARTER), first_staging(m, q * QUARTER, QUARTER), ACT.Copy,
                               scale=w_scale[:, m:m + 1]).then_inc(fhi_ready, 1)

            def split_later(piece, h):
                act.wait_ge(wscale_ready, piece.matrix + 1)
                act.activation(w_at(piece.k + 1, piece.kind, HI, h * HALF, HALF), stage[:, h * HALF:(h + 1) * HALF],
                               ACT.Copy, scale=w_scale[:, 2:3]).then_inc(whi_ready, 1)

            def split_x(s):
                act.wait_ge(xscale_ready, s.at + 1)
                if s.since(2):
                    act.wait_ge(xT_hi_done, s.at - 1)
                act.activation(x16[:, s.buf(2), HI, :], xs[:, s.buf(XRING), :], ACT.Copy,
                               scale=xst[:, s.buf(UNROLL), 3:4]).then_inc(xhi_ready, 1)

            def copy_xT_hi(s):
                act.wait_ge(xT_hi_done, s.at + 1)
                if s.since(2):
                    act.wait_ge(z_done, s.at - 1)
                act.copy(xT[:, s.buf(2), HI, :, :], xT_ps[:, HI, :, :]).then_inc(xT_hi_ready, 1)

            def copy_xT_lo(s):
                act.wait_ge(xT_lo_done, s.at + 1)
                act.copy(xT[:, s.buf(2), LO, :, :], xT_ps[:, LO, :, :]).then_inc(xT_lo_ready, 1)

            def normalise(s):
                act.wait_ge(norm_ready, s.at + 1)
                row = ys[:, s.buf(YRING), :]
                act.activation(row, row, ACT.Identity, bias=norm[:, s.buf(UNROLL), 3:4],
                               scale=norm[:, s.buf(UNROLL), 1:2]).then_inc(yn_ready, 1)

            def gelu(s):
                act.wait_ge(z_ready, s.at + 1)
                act.activation(hs[:, s.buf(2), :], hs[:, s.buf(2), :], ACT.Gelu).then_inc(h_ready, 1)

            def copy_hT(s):
                act.wait_ge(hT_done, s.at + 1)
                if s.since(2):
                    act.wait_ge(u_done, s.at - 1)
                act.copy(hT[:, s.buf(2), :, :, :], hT_ps[:, :, :, :]).then_inc(hT_ready, 1)

            def split_h(s):
                act.wait_ge(hscale_ready, s.at + 1)
                if s.since(2):
                    act.wait_ge(hT_done, s.at - 1)
                act.activation(h16[:, s.buf(2), HI, :], hs[:, s.buf(2), :], ACT.Copy,
                               scale=hst[:, s.buf(UNROLL), 3:4]).then_inc(hhi_ready, 1)

            def scale_in_place(q):
                act.wait_ge(fscale_ready, UP + 1)
                v = first_staging(UP, q * QUARTER, QUARTER)
                act.activation(v, v, ACT.Copy, scale=w_scale[:, UP:UP + 1]).then_inc(up_scaled, 1)
                act.wait_ge(up_scaled, q - 1)
                act.copy(w_at(0, UP, HI, q * QUARTER, QUARTER), v).then_inc(fhi_ready, 1)

            def first_step():
                split_x(Slot(0, 2))
                gelu(Slot(0, 0))
                split_h(Slot(0, 0))
                copy_xT_hi(Slot(0, 2))
                copy_xT_lo(Slot(0, 2))

            def second_step():
                gelu(Slot(0, 1))
                split_first(UP, 0)
                copy_hT(Slot(0, 0))
                split_first(UP, 1)
                split_x(Slot(0, 3))
                scale_in_place(2)
                split_h(Slot(0, 1))
                scale_in_place(3)

            def step(s, piece):
                if not s.loop and s.c < 2:
                    (first_step, second_step)[s.c]()
                    return
                if (s + 2).before(N):
                    split_x(s + 2)
                if s.before(N):
                    gelu(s)
                if (s + 1).before(N):
                    copy_xT_hi(s + 1)
                    copy_xT_lo(s + 1)
                if not s.before(N) and (s - 1).before(N):
                    copy_hT(s - 1)
                if s.since(3) and (s - 3).before(N - 2):
                    normalise(s - 3)
                if s.before(N):
                    split_h(s)
                    copy_hT(s - 1)
                if piece is not None and piece.phase in (3, 4):
                    split_later(piece, piece.phase - 3)

            act.wait_ge(consts_ready, 2)
            act.activation(warm[:, :], eps[:, :], ACT.Gelu)
            split_first(DOWN, 0)
            split_x(Slot(0, 0))
            split_first(DOWN, 1)
            copy_xT_hi(Slot(0, 0))
            copy_xT_lo(Slot(0, 0))
            split_first(DOWN, 2)
            split_x(Slot(0, 1))
            split_first(DOWN, 3)
            copy_xT_hi(Slot(0, 1))
            copy_xT_lo(Slot(0, 1))
            steps(act, step, N + 3)

        @block.vector
        def _(dve):
            chained = [0]

            def link(ins):
                chained[0] += 1
                ins.then_inc(chain, 1)
                dve.wait_ge(chain, chained[0])

            def rank_roles():
                link(dve.memset(role_keys[:, 0, :], -1.0))
                dve.wait_ge(counting_ready, 2)
                link(dve.tensor_copy(counting_f[:, :], counting[:, :]))
                dve.wait_ge(roles_loaded, DMA)
                link(dve.tensor_scalar(role_f[:, 0, :], role_in[:, :], 0.0, float(R), ALU.is_lt, ALU.mult))
                link(dve.tensor_tensor(role_f[:, 1, :], role_in[:, :], role_f[:, 0, :], ALU.add))
                link(dve.tensor_scalar(role_f[:, 2, :], role_f[:, 1, :], 0.0, float(R - 1), ALU.max, ALU.min))
                for r in range(R):
                    link(dve.tensor_scalar(is_role[:, r, :], role_f[:, 2, :], float(r), None, ALU.is_equal))
                link(dve.tensor_reduce(per_role[:, :], is_role[:, :, :], AX_X, ALU.add))
                link(dve.scalar_tensor_tensor(out=role_keys[:, 0, 0:R], in0=per_role[:, :], scalar=4.0 * N,
                                              in1=counting_f[:, N:N + R], op0=ALU.mult, op1=ALU.add))
                link(dve.max(role_keys[:, 1, :], role_keys[:, 0, :]))
                link(dve.tensor_copy(top_role[:, :], role_keys[:, 1, 0:R]))
                dve.tensor_scalar(role_by_rank[:, :], top_role[:, :], N.bit_length() - 1, 3,
                                  ALU.logical_shift_right, ALU.bitwise_and).then_inc(ranked, 1)

            def sort_sequences():
                before = counting_f[:, 0:N]
                for r in range(R):
                    link(dve.scalar_tensor_tensor(out=keys[:, r, :], in0=is_role[:, r, :],
                                                  scalar=role_keys[:, 0, r:r + 1], in1=before,
                                                  op0=ALU.mult, op1=ALU.add))
                    before = keys[:, r, :]
                for g in range(N // 8):
                    top = sorted_keys[:, 0, 8 * g:8 * g + 8]
                    now, then = keys[:, R - 1 + g % 2, :], keys[:, R - (g % 2), :]
                    link(dve.max(top, now))
                    if g + 1 < N // 8:
                        link(dve.match_replace(then, top, now, -1e9))
                key, later = sorted_keys[:, 0, :], sorted_keys[:, 1, :]
                link(dve.tensor_scalar(later, key, role_keys[:, 1, 0:1], None, ALU.is_lt))
                link(dve.scalar_tensor_tensor(out=rank_at[:, :], in0=key, scalar=role_keys[:, 1, 1:2], in1=later,
                                              op0=ALU.is_lt, op1=ALU.add))
                link(dve.tensor_copy(top_seq[:, :], key))
                dve.tensor_scalar(seq_at[:, :], top_seq[:, :], N - 1, None, ALU.bitwise_and).then_inc(sorted_ready, 1)

            def power_scales(count, top, power, inverse, scale, pow_ready, inv_ready, scale_ready):
                dve.tensor_scalar(power.bitcast(I32), top.bitcast(I32), EXPONENT_BITS, None, ALU.bitwise_and
                                  ).then_inc(pow_ready, 1)
                dve.wait_ge(pow_ready, count)
                dve.tensor_scalar(inverse, power, TINIEST, 1.0 / TOP, ALU.max, ALU.mult).then_inc(inv_ready, 1)
                dve.wait_ge(inv_ready, count)
                dve.reciprocal(scale, inverse).then_inc(scale_ready, 1)

            def largest_first(m, q):
                dve.wait_ge(first_loaded[m][q], DMA)
                dve.tensor_reduce(first_max[:, m, q:q + 1], first_staging(m, q * QUARTER, QUARTER), AX_X, ALU.max,
                                  apply_absolute_value=True).then_inc(fmax_ready, 1)

            def scale_first(m):
                dve.wait_ge(fall_ready, m + 1)
                dve.tensor_reduce(wpow[:, 0:1], first_all[:, m, :], AX_X, ALU.max).then_inc(ftop_ready, 1)
                dve.wait_ge(ftop_ready, m + 1)
                power_scales(m + 1, wpow[:, 0:1], wpow[:, 1:2], w_inv[:, m:m + 1], w_scale[:, m:m + 1],
                             fpow_ready, finv_ready, fscale_ready)

            def split_first(m, q):
                dve.wait_ge(fhi_ready, 4 * m + q + 1)
                dve.scalar_tensor_tensor(out=w_at(0, m, LO, q * QUARTER, QUARTER),
                                         in0=first_staging(m, q * QUARTER, QUARTER), scalar=w_scale[:, m:m + 1],
                                         in1=w_at(0, m, HI, q * QUARTER, QUARTER), op0=ALU.mult, op1=ALU.subtract
                                         ).then_inc(wlo_ready, 1)

            def largest_later(piece, h):
                dve.wait_ge(w_loaded[h], piece.matrix * DMA + DMA)
                dve.tensor_reduce(wmax[:, h:h + 1], stage[:, h * HALF:(h + 1) * HALF], AX_X, ALU.max,
                                  apply_absolute_value=True).then_inc(wmax_ready, 1)

            def scale_later(piece):
                dve.wait_ge(wall_ready, piece.matrix + 1)
                dve.tensor_reduce(wpow[:, 0:1], wall[:, :], AX_X, ALU.max).then_inc(wtop_ready, 1)
                dve.wait_ge(wtop_ready, piece.matrix + 1)
                power_scales(piece.matrix + 1, wpow[:, 0:1], wpow[:, 1:2], wpow[:, 2:3], w_scale[:, 2:3],
                             wpow_ready, winv_ready, wscale_ready)
                dve.tensor_copy(w_inv[:, bass.ds(piece.matrix + 2, 1)], wpow[:, 2:3]).then_inc(wtable_ready, 1)

            def split_later(piece, h):
                if h == 0:
                    dve.wait_ge(wtable_ready, piece.matrix + 1)
                dve.wait_ge(whi_ready, piece.matrix * 2 + h + 1)
                dve.scalar_tensor_tensor(out=w_at(piece.k + 1, piece.kind, LO, h * HALF, HALF),
                                         in0=stage[:, h * HALF:(h + 1) * HALF], scalar=w_scale[:, 2:3],
                                         in1=w_at(piece.k + 1, piece.kind, HI, h * HALF, HALF),
                                         op0=ALU.mult, op1=ALU.subtract).then_inc(wlo_ready, 1)

            def largest_x(s):
                dve.wait_ge(x_loaded[s.buf(XRING)], s.turn(XRING) * DMA + DMA)
                dve.tensor_reduce(xst[:, s.buf(UNROLL), 0:1], xs[:, s.buf(XRING), :], AX_X, ALU.max,
                                  apply_absolute_value=True).then_inc(xmax_ready, 1)

            def scale_x(s):
                st = xst[:, s.buf(UNROLL), :]
                dve.wait_ge(xmax_ready, s.at + 1)
                power_scales(s.at + 1, st[:, 0:1], st[:, 1:2], st[:, 2:3], st[:, 3:4],
                             xpow_ready, xinv_ready, xscale_ready)

            def split_x(s):
                dve.wait_ge(xhi_ready, s.at + 1)
                if s.since(2):
                    dve.wait_ge(xT_lo_done, s.at - 1)
                dve.scalar_tensor_tensor(out=x16[:, s.buf(2), LO, :], in0=xs[:, s.buf(XRING), :],
                                         scalar=xst[:, s.buf(UNROLL), 3:4], in1=x16[:, s.buf(2), HI, :],
                                         op0=ALU.mult, op1=ALU.subtract).then_inc(xlo_ready, 1)

            def make_z(s):
                rank = dve.value_load(rank_at[0:1, bass.ds(s.at, 1)], min_val=0, max_val=R - 1)
                j = s.buf(UNROLL)
                dve.tensor_tensor(undo[:, j, 0:1], xst[:, j, 2:3], w_inv[:, bass.ds(rank * 2 + DOWN, 1)], ALU.mult
                                  ).then_inc(zundo_ready, 1)
                dve.wait_ge(zundo_ready, s.at + 1)
                if s.since(2):
                    dve.wait_ge(hhi_ready, s.at - 1)
                dve.wait_ge(z_done, s.at + 1)
                dve.scalar_tensor_tensor(out=hs[:, s.buf(2), :], in0=z_ps[:, s.buf(2), :], scalar=undo[:, j, 0:1],
                                         in1=bdown_all[:, bass.ds(rank * K, K)], op0=ALU.mult, op1=ALU.add
                                         ).then_inc(z_ready, 1)

            def scale_h(s):
                j = s.buf(UNROLL)
                dve.wait_ge(h_ready, s.at + 1)
                dve.tensor_reduce(hst[:, j, 0:1], hs[:, s.buf(2), :], AX_X, ALU.max, apply_absolute_value=True
                                  ).then_inc(hmax_ready, 1)
                dve.wait_ge(hmax_ready, s.at + 1)
                power_scales(s.at + 1, hst[:, j, 0:1], hst[:, j, 1:2], hst[:, j, 2:3], hst[:, j, 3:4],
                             hpow_ready, hinv_ready, hscale_ready)

            def split_h(s):
                dve.wait_ge(hhi_ready, s.at + 1)
                dve.scalar_tensor_tensor(out=h16[:, s.buf(2), LO, :], in0=hs[:, s.buf(2), :],
                                         scalar=hst[:, s.buf(UNROLL), 3:4], in1=h16[:, s.buf(2), HI, :],
                                         op0=ALU.mult, op1=ALU.subtract).then_inc(hlo_ready, 1)

            def make_y(s):
                rank = dve.value_load(rank_at[0:1, bass.ds(s.at, 1)], min_val=0, max_val=R - 1)
                j = s.buf(UNROLL)
                dve.tensor_tensor(undo[:, j, 1:2], hst[:, j, 2:3], w_inv[:, bass.ds(rank * 2 + UP, 1)], ALU.mult
                                  ).then_inc(uundo_ready, 1)
                dve.wait_ge(uundo_ready, s.at + 1)
                last = not s.before(N - 1)
                if not last:
                    dve.wait_ge(u_done, s.at + 1)
                dve.wait_ge(xres_ready, s.at + 1)
                if s.since(YRING):
                    dve.wait_ge(stored[s.buf(YRING)], s.turn(YRING) * DMA)
                y, u, row = ys[:, s.buf(YRING), :], u_banks(s), xs[:, s.buf(XRING), :]
                if last:
                    for c in range(H // BANK):
                        cols = slice(c * BANK, (c + 1) * BANK)
                        dve.wait_ge(last_u_done, c + 1)
                        dve.scalar_tensor_tensor(out=y[:, cols], in0=u[:, cols], scalar=undo[:, j, 1:2],
                                                 in1=row[:, cols], op0=ALU.mult, op1=ALU.add).then_inc(last_y_ready, 1)
                        dve.wait_ge(last_y_ready, c + 1)
                        dve.bn_stats(stats[:, j, c, :], y[:, cols]).then_inc(stats_ready, 1)
                    return
                dve.scalar_tensor_tensor(out=y, in0=u, scalar=undo[:, j, 1:2], in1=row, op0=ALU.mult, op1=ALU.add
                                         ).then_inc(y_ready, 1)
                dve.wait_ge(y_ready, s.at + 1)
                for c in range(H // BANK):
                    dve.bn_stats(stats[:, j, c, :], y[:, c * BANK:(c + 1) * BANK]).then_inc(stats_ready, 1)

            def scale_last(s):
                rank = dve.value_load(rank_at[0:1, bass.ds(s.at, 1)], min_val=0, max_val=R - 1)
                j, y = s.buf(UNROLL), ys[:, s.buf(YRING), :]
                dve.wait_ge(moments_ready, s.at + 1)
                for c in range(2):
                    cols = y[:, c * BANK:(c + 1) * BANK]
                    dve.scalar_tensor_tensor(out=cols, in0=cols, scalar=moments[:, j, 0:1],
                                             in1=gamma_all[:, bass.ds(rank * H + c * BANK, BANK)],
                                             op0=ALU.subtract, op1=ALU.mult).then_inc(last_scaled, 1)

            def finish_last(s):
                rank = dve.value_load(rank_at[0:1, bass.ds(s.at, 1)], min_val=0, max_val=R - 1)
                j, before = s.buf(UNROLL), (s.c - (N - 2)) * 2
                y = ys[:, s.buf(YRING), :]
                dve.wait_ge(rstd_ready, s.at + 1)
                for c in range(2):
                    cols = y[:, c * BANK:(c + 1) * BANK]
                    dve.wait_ge(last_scaled, before + c + 1)
                    dve.scalar_tensor_tensor(out=cols, in0=cols, scalar=norm[:, j, 1:2],
                                             in1=beta_all[:, bass.ds(rank * H + c * BANK, BANK)],
                                             op0=ALU.mult, op1=ALU.add).then_inc(last_result_ready, 1)

            def make_moments(s):
                j = s.buf(UNROLL)
                dve.bn_aggr(moments[:, j, :], stats[:, j, :, :]).then_inc(moments_ready, 1)

            def first_step():
                largest_x(Slot(0, 2))
                scale_x(Slot(0, 2))
                largest_first(UP, 0)
                make_z(Slot(0, 0))
                split_x(Slot(0, 2))
                scale_h(Slot(0, 0))
                largest_first(UP, 1)
                largest_first(UP, 2)
                split_h(Slot(0, 0))
                largest_first(UP, 3)

            def second_step():
                make_z(Slot(0, 1))
                scale_first(UP)
                largest_x(Slot(0, 3))
                split_first(UP, 0)
                scale_x(Slot(0, 3))
                split_first(UP, 1)
                scale_h(Slot(0, 1))
                split_x(Slot(0, 3))
                split_h(Slot(0, 1))

            def step(s, piece):
                if not s.loop and s.c < 2:
                    (first_step, second_step)[s.c]()
                    return
                if not s.loop and s.c == PEELED - 1:
                    dve.wait_ge(late_tables_loaded, (R - 1) * 4 * DMA)
                if not s.before(N) and (s - 1).before(N):
                    split_h(s - 1)
                if s.since(3):
                    make_y(s - 3)
                if s.since(3) and s.before(N):
                    split_h(s - 1)
                if s.since(3):
                    dve.wait_ge(stats_ready, (s - 3).at * 2 + 2)
                if (s + 2).before(N):
                    largest_x(s + 2)
                if s.since(3):
                    make_moments(s - 3)
                if not (s - 3).before(N - 2):
                    scale_last(s - 3)
                if not (s - 3).before(N - 1):
                    finish_last(s - 4)
                    finish_last(s - 3)
                if (s + 2).before(N):
                    scale_x(s + 2)
                if piece is not None and piece.phase == 3:
                    scale_later(piece)
                if s.before(N):
                    make_z(s)
                if piece is not None and piece.phase in (1, 2):
                    largest_later(piece, piece.phase - 1)
                if (s + 2).before(N):
                    split_x(s + 2)
                if s.before(N):
                    scale_h(s)
                if piece is not None and piece.phase in (4, 5):
                    split_later(piece, piece.phase - 4)

            rank_roles()
            sort_sequences()
            for q in range(4):
                largest_first(DOWN, q)
            scale_first(DOWN)
            largest_x(Slot(0, 0))
            scale_x(Slot(0, 0))
            split_first(DOWN, 0)
            split_x(Slot(0, 0))
            split_first(DOWN, 1)
            largest_x(Slot(0, 1))
            scale_x(Slot(0, 1))
            split_first(DOWN, 2)
            split_x(Slot(0, 1))
            split_first(DOWN, 3)
            dve.wait_ge(bdown_loaded, DMA)
            steps(dve, step, N + 3)

        @block.tensor
        def _(pe):
            pe.wait_ge(ident_ready, 1)
            pe.wait_ge(sorted_ready, 1)

            def transpose_x(s):
                for part, taken, copied, done in ((HI, xhi_ready, xT_hi_ready, xT_hi_done),
                                                  (LO, xlo_ready, xT_lo_ready, xT_lo_done)):
                    pe.wait_ge(taken, s.at + 1)
                    if s.since(1):
                        pe.wait_ge(copied, s.at)
                    for c in range(HC):
                        t = pe.transpose(xT_ps[:, part, c, :], x16[:, s.buf(2), part, c * P:(c + 1) * P], ident[:, :])
                    t.then_inc(done, 1)

            def transpose_h(s):
                pe.wait_ge(hlo_ready, s.at + 1)
                if s.since(1):
                    pe.wait_ge(hT_ready, s.at)
                for part in (HI, LO):
                    for c in range(KC):
                        t = pe.transpose(hT_ps[:, part, c, :], h16[:, s.buf(2), part, c * P:(c + 1) * P], ident[:, :])
                t.then_inc(hT_done, 1)

            def down(s):
                rank = pe.value_load(rank_at[0:1, bass.ds(s.at, 1)], min_val=0, max_val=R - 1)
                if s.since(2):
                    pe.wait_ge(z_ready, s.at - 1)
                pe.wait_ge(xT_lo_ready, s.at + 1)
                for c in range(HC):
                    if not s.loop and s.c < 2 and c == HC // 2:
                        transpose_x(s + 1)
                    if not s.loop and s.c == 0 and c % 2 == 0:
                        pe.wait_ge(wlo_ready, c // 2 + 1)
                    for a, w in PASSES:
                        t = pe.matmul(z_ps[:, s.buf(2), :], xT[:, s.buf(2), a, c, :], w_at(rank, DOWN, w, c * K, K),
                                      start=(c == 0 and a == HI and w == HI), stop=(c == HC - 1 and a == LO))
                t.then_inc(z_done, 1)

            def up(s):
                rank = pe.value_load(rank_at[0:1, bass.ds(s.at, 1)], min_val=0, max_val=R - 1)
                u = u_banks(s)
                if not s.before(N - 1):
                    pe.wait_ge(y_ready, s.at - 1)
                elif not s.before(N - 2):
                    pe.wait_ge(z_ready, N)
                elif s.since(1):
                    pe.wait_ge(y_ready, s.at)
                pe.wait_ge(hT_ready, s.at + 1)
                if s.before(N - 1):
                    order = [(c, a, w, n) for c in range(KC) for a, w in PASSES for n in range(H // BANK)]
                else:
                    order = [(c, a, w, n) for n in range(H // BANK) for c in range(KC) for a, w in PASSES]
                for c, a, w, n in order:
                    if not s.loop and s.c == 0 and (c, a, w, n) == (KC // 2, HI, HI, 0):
                        transpose_h(s + 1)
                        transpose_x(s + 3)
                    if not s.loop and s.c == 0 and (a, w, n) == (HI, HI, 0):
                        pe.wait_ge(*((wlo_ready, 4 + c + 1) if c < 2 else (up_lo_ready, c - 1)))
                    t = pe.matmul(u[:, n * BANK:(n + 1) * BANK], hT[:, s.buf(2), a, c, :],
                                  w_at(rank, UP, w, c * H + n * BANK, BANK),
                                  start=(c == 0 and a == HI and w == HI), stop=(c == KC - 1 and a == LO))
                    if not s.before(N - 1) and (c, a) == (KC - 1, LO):
                        t.then_inc(last_u_done, 1)
                if s.before(N - 1):
                    t.then_inc(u_done, 1)

            def step(s, piece):
                if piece is not None and piece.kind == UP and piece.phase == 0:
                    pe.wait_ge(wlo_ready, piece.k * 4 + FIRST)
                if s.loop and piece is None and s.c == LOOP_B + UNROLL - 1:
                    pe.wait_ge(wlo_ready, FIRST + 4 * (R - 1))
                if s.before(N):
                    down(s)
                if s.since(1) and (s - 1).before(N) and (s.loop or s.c != 2):
                    transpose_h(s - 1)
                if s.since(3) and (s + 1).before(N):
                    transpose_x(s + 1)
                if s.since(2):
                    up(s - 2)

            pe.wait_ge(fmax_ready, 4)
            for _ in range(32):
                pe.matmul(u_ps[:, 0:P], ident[:, :], ident[:, :], start=True, stop=True)
            transpose_x(Slot(0, 0))
            steps(pe, step, N + 2)


_INS = ["x", "itok_B_1_2", "L0_cond_W_down", "L0_cond_b_down", "L0_cond_W_up", "L0_cond_b_up",
        "L0_cond_gamma", "L0_cond_beta"]
_OUT = ((64, 128, 1024), "float32")


def kernel(**inputs):
    import numpy as _np
    import concourse.bacc as _bacc
    from concourse import mybir as _mybir
    from concourse.bass_utils import run_bass_kernel_spmd as _run

    nc = _bacc.Bacc("TRN2", target_bir_lowering=False, num_devices=1,
                    dynamic_dma_scratch_size=1024)
    arrays, args = {}, []
    for name in _INS:
        a = _np.ascontiguousarray(inputs[name])
        arrays[f"in_{name}_dram"] = a
        args.append(nc.dram_tensor(f"in_{name}_dram", a.shape, _mybir.dt.from_np(a.dtype), kind="ExternalInput").ap())
    shape, dtype = _OUT
    args.append(nc.dram_tensor("out_0_dram", shape, _mybir.dt.from_np(_np.dtype(dtype)), kind="ExternalOutput").ap())
    adapter(nc, *args)
    r = _run(nc, [arrays], core_ids=[0])
    return r.results[0]["out_0_dram"]
```
